# Optimizing a Trainium2 kernel written in Bass

```python
import numpy as np
import jax
import jax.numpy as jnp

def _softmax(x, axis=-1):
    return jax.nn.softmax(x, axis=axis)

def _gelu(x):
    return jax.nn.gelu(x, approximate=True)

def _silu(x):
    return jax.nn.silu(x)

def _sigmoid(x):
    return jax.nn.sigmoid(x)

def _layernorm(x, axis=-1, eps=1e-05):
    m = jnp.mean(x, axis=axis, keepdims=True)
    v = jnp.var(x, axis=axis, keepdims=True)
    return (x - m) / jnp.sqrt(v + eps)

def _scatter_add(tgt, idx, src, axis=0):
    return tgt.at[idx].add(src)

def _segment_sum(src, seg, n):
    return jax.ops.segment_sum(src, seg, n)
kernel_name = 'mk_decoder_postln_d1_seqx_r8_1dbfed'

def setup_inputs(seed: int=0):
    np.random.seed(seed)
    _w = jnp.asarray

    def _rec_inputs():
        import jax
        import jax.numpy as jnp
        _rk = jax.random.key(seed)
        x = -0.0002928 + 1 * jax.random.normal(jax.random.fold_in(_rk, 1), (32, 128, 128), jnp.float32)
        _lenS = 128 - jax.random.randint(jax.random.fold_in(_rk, 7), (32,), 0, max(1, 128 // 4) + 1, jnp.int32)
        _lenS2 = 128 - jax.random.randint(jax.random.fold_in(_rk, 8), (32,), 0, max(1, 128 // 4) + 1, jnp.int32)
        _ctx_1024P = jax.random.normal(jax.random.fold_in(_rk, 11), (32, 16, 128), jnp.float32)
        _ctx_1024c = jax.random.dirichlet(jax.random.fold_in(_rk, 511), 0.3 * jnp.ones((16,), jnp.float32), (32, 128))
        _ctx_1024t = jnp.einsum('bsk,bkd->bsd', _ctx_1024c, _ctx_1024P)
        _ctx_1024t = _ctx_1024t * jax.lax.rsqrt(jnp.mean(jnp.square(_ctx_1024t)) + 1e-12) * 0.953939
        ctx_1024 = -1.39393e-06 + 0.999914 * (_ctx_1024t + 0.3 * jax.random.normal(jax.random.fold_in(_rk, 611), (32, 128, 128), jnp.float32))
        return (x, ctx_1024)
    x, ctx_1024 = _rec_inputs()

    def _L0_attn_setup():
        import jax, jax.numpy as jnp
        import numpy as np
        CHUNK = 32
        ROPE_BASE = 10000.0
        EPS = 1e-06

        def _rmsnorm(x, scale):
            xf = x.astype(jnp.float32)
            rms = jax.lax.rsqrt(jnp.mean(xf * xf, axis=-1, keepdims=True) + EPS)
            out = scale.astype(jnp.float32) * (xf * rms)
            return jnp.clip(out, -60000.0, 60000.0).astype(x.dtype)

        def _rope(v, N, d_head, dtype):
            half = d_head // 2
            inv_freq = 1.0 / ROPE_BASE ** (jnp.arange(0, d_head, 2, dtype=jnp.float32) / d_head)
            freqs = jnp.arange(N, dtype=jnp.float32)[:, None] * inv_freq[None, :]
            cos = jnp.cos(freqs).astype(dtype)[None, :, None, :]
            sin = jnp.sin(freqs).astype(dtype)[None, :, None, :]
            v1, v2 = (v[..., :half], v[..., half:])
            return jnp.concatenate([v1 * cos - v2 * sin, v1 * sin + v2 * cos], axis=-1)
        key = jax.random.key(seed)
        ks = jax.random.split(key, 8)
        B, N, D, H, K = (4, 1024, 128, 16, 4)
        x = jax.random.normal(ks[0], (B, N, D), dtype=jnp.float32)
        norm_scale = jnp.ones((D,), dtype=jnp.float32)
        conv_w = jax.random.normal(ks[1], (D, 1, K), dtype=jnp.float32) * 0.2
        conv_b = jax.random.normal(ks[2], (D,), dtype=jnp.float32) * 0.02
        in_proj_w = jax.random.normal(ks[3], (D, 3 * D), dtype=jnp.float32) * 0.02
        dt_bias = jax.random.normal(ks[4], (D,), dtype=jnp.float32) * 0.5
        head_mix = jnp.eye(H, dtype=jnp.float32) + 0.02 * jax.random.normal(ks[5], (H, H), dtype=jnp.float32)
        out_proj_w = jax.random.normal(ks[6], (D, D), dtype=jnp.float32) * 0.02
        return {'x': x, 'norm_scale': norm_scale, 'conv_w': conv_w, 'conv_b': conv_b, 'in_proj_w': in_proj_w, 'dt_bias': dt_bias, 'head_mix': head_mix, 'out_proj_w': out_proj_w}
    _L0_attn_all = _L0_attn_setup()
    _L0_attn_in = {k: v for k, v in _L0_attn_all.items() if k in ('norm_scale', 'conv_w', 'conv_b', 'in_proj_w', 'dt_bias', 'head_mix', 'out_proj_w')}
    del _L0_attn_all

    def _L0_xattn_setup():
        import jax, jax.numpy as jnp
        import numpy as np
        D_MODEL = 128
        N_HEADS = 16
        D_K = D_MODEL // N_HEADS
        key = jax.random.key(seed)
        ks = jax.random.split(key, 11)
        B, L = (2, 256)
        s = 1.0 / np.sqrt(D_MODEL)
        return {'queries': jax.random.normal(ks[0], (B, L, D_MODEL), jnp.float32), 'keys': jax.random.normal(ks[1], (B, L, D_MODEL), jnp.float32), 'values': jax.random.normal(ks[2], (B, L, D_MODEL), jnp.float32), 'Wq': jax.random.normal(ks[3], (D_MODEL, D_MODEL), jnp.float32) * s, 'bq': jnp.zeros((D_MODEL,), jnp.float32), 'Wk': jax.random.normal(ks[4], (D_MODEL, D_MODEL), jnp.float32) * s, 'bk': jnp.zeros((D_MODEL,), jnp.float32), 'Wv': jax.random.normal(ks[5], (D_MODEL, D_MODEL), jnp.float32) * s, 'bv': jnp.zeros((D_MODEL,), jnp.float32), 'Wo': jax.random.normal(ks[6], (D_MODEL, D_MODEL), jnp.float32) * s, 'bo': jnp.zeros((D_MODEL,), jnp.float32)}
    _L0_xattn_all = _L0_xattn_setup()
    _L0_xattn_in = {k: v for k, v in _L0_xattn_all.items() if k in ('Wq', 'bq', 'Wk', 'bk', 'Wv', 'bv', 'Wo', 'bo')}
    del _L0_xattn_all

    def _L0_ffn_setup():
        import jax, jax.numpy as jnp
        import numpy as np

        def fixed_quant(x, width, frac_width):
            scale = jnp.float32(2.0 ** frac_width)
            imax = jnp.float32(2 ** (width - 1) - 1)
            imin = jnp.float32(-2 ** (width - 1))
            return jnp.clip(jnp.round(x * scale), imin, imax) / scale
        IN_F, HID_F, OUT_F = (128, 512, 128)
        B, S = (4, 256)
        ACT_Q = (8, 4)
        W_Q = (8, 6)
        BIAS_Q = (8, 6)

        def quantized_linear(x, w, b):
            xq = fixed_quant(x, *ACT_Q)
            wq = fixed_quant(w, *W_Q)
            bq = fixed_quant(b, *BIAS_Q)
            return jnp.einsum('bsi,oi->bso', xq, wq) + bq

        def quantized_relu(x):
            return jax.nn.relu(fixed_quant(x, *ACT_Q))
        key = jax.random.key(seed)
        k_x, k_w1, k_b1, k_w2, k_b2 = jax.random.split(key, 5)
        x = jax.random.normal(k_x, (B, S, IN_F), dtype=jnp.float32)
        w1 = jax.random.normal(k_w1, (HID_F, IN_F), dtype=jnp.float32) / np.sqrt(IN_F)
        b1 = jax.random.normal(k_b1, (HID_F,), dtype=jnp.float32) / np.sqrt(IN_F)
        w2 = jax.random.normal(k_w2, (OUT_F, HID_F), dtype=jnp.float32) / np.sqrt(HID_F)
        b2 = jax.random.normal(k_b2, (OUT_F,), dtype=jnp.float32) / np.sqrt(HID_F)
        return {'x': x, 'w1': w1, 'b1': b1, 'w2': w2, 'b2': b2}
    _L0_ffn_all = _L0_ffn_setup()
    _L0_ffn_in = {k: v for k, v in _L0_ffn_all.items() if k in ('w1', 'b1', 'w2', 'b2')}
    del _L0_ffn_all
    return {'x': x, 'ctx_1024': ctx_1024, 'L0_attn_norm_scale': _L0_attn_in['norm_scale'], 'L0_attn_conv_w': _L0_attn_in['conv_w'], 'L0_attn_conv_b': _L0_attn_in['conv_b'], 'L0_attn_in_proj_w': _L0_attn_in['in_proj_w'], 'L0_attn_dt_bias': _L0_attn_in['dt_bias'], 'L0_attn_head_mix': _L0_attn_in['head_mix'], 'L0_attn_out_proj_w': _L0_attn_in['out_proj_w'], 'L0_xattn_Wq': _L0_xattn_in['Wq'], 'L0_xattn_bq': _L0_xattn_in['bq'], 'L0_xattn_Wk': _L0_xattn_in['Wk'], 'L0_xattn_bk': _L0_xattn_in['bk'], 'L0_xattn_Wv': _L0_xattn_in['Wv'], 'L0_xattn_bv': _L0_xattn_in['bv'], 'L0_xattn_Wo': _L0_xattn_in['Wo'], 'L0_xattn_bo': _L0_xattn_in['bo'], 'L0_ffn_w1': _L0_ffn_in['w1'], 'L0_ffn_b1': _L0_ffn_in['b1'], 'L0_ffn_w2': _L0_ffn_in['w2'], 'L0_ffn_b2': _L0_ffn_in['b2']}

def reference(x, ctx_1024, L0_attn_norm_scale, L0_attn_conv_w, L0_attn_conv_b, L0_attn_in_proj_w, L0_attn_dt_bias, L0_attn_head_mix, L0_attn_out_proj_w, L0_xattn_Wq, L0_xattn_bq, L0_xattn_Wk, L0_xattn_bk, L0_xattn_Wv, L0_xattn_bv, L0_xattn_Wo, L0_xattn_bo, L0_ffn_w1, L0_ffn_b1, L0_ffn_w2, L0_ffn_b2):
    import jax
    import jax.numpy as jnp

    def _L0_attn_ref(x, norm_scale, conv_w, conv_b, in_proj_w, dt_bias, head_mix, out_proj_w):
        import jax, jax.numpy as jnp
        import numpy as np
        CHUNK = 32
        ROPE_BASE = 10000.0
        EPS = 1e-06

        def _rmsnorm(x, scale):
            xf = x.astype(jnp.float32)
            rms = jax.lax.rsqrt(jnp.mean(xf * xf, axis=-1, keepdims=True) + EPS)
            out = scale.astype(jnp.float32) * (xf * rms)
            return jnp.clip(out, -60000.0, 60000.0).astype(x.dtype)

        def _rope(v, N, d_head, dtype):
            half = d_head // 2
            inv_freq = 1.0 / ROPE_BASE ** (jnp.arange(0, d_head, 2, dtype=jnp.float32) / d_head)
            freqs = jnp.arange(N, dtype=jnp.float32)[:, None] * inv_freq[None, :]
            cos = jnp.cos(freqs).astype(dtype)[None, :, None, :]
            sin = jnp.sin(freqs).astype(dtype)[None, :, None, :]
            v1, v2 = (v[..., :half], v[..., half:])
            return jnp.concatenate([v1 * cos - v2 * sin, v1 * sin + v2 * cos], axis=-1)
        residual = x
        B, N, D = x.shape
        H = head_mix.shape[0]
        d_head = D // H
        xn = _rmsnorm(x, norm_scale)
        K = conv_w.shape[-1]
        xc = jax.lax.conv_general_dilated(xn.transpose(0, 2, 1), conv_w, window_strides=(1,), padding=[(K - 1, 0)], feature_group_count=D, dimension_numbers=('NCH', 'OIH', 'NCH'))
        xc = (xc + conv_b[None, :, None]).transpose(0, 2, 1)
        xc = xc * jax.nn.sigmoid(xc)
        fused = xc @ in_proj_w
        dt_raw, v, gate_raw = jnp.split(fused, 3, axis=-1)
        dt = jnp.clip(jax.nn.softplus(dt_raw.astype(jnp.float32) + dt_bias.astype(jnp.float32)), 0.001, 2.0).astype(dt_raw.dtype)
        gate = jax.nn.sigmoid(gate_raw)
        log_alpha = -dt.astype(jnp.float32)
        v_rot = _rope(v.reshape(B, N, H, d_head), N, d_head, x.dtype).reshape(B, N, D)
        v_in = (v_rot * dt).astype(jnp.float32)
        pad = -N % CHUNK
        if pad:
            v_in = jnp.pad(v_in, ((0, 0), (0, pad), (0, 0)))
            log_alpha = jnp.pad(log_alpha, ((0, 0), (0, pad), (0, 0)))
        Np = N + pad
        nc = Np // CHUNK
        v_ch = v_in.reshape(B, nc, CHUNK, D)
        la_ch = log_alpha.reshape(B, nc, CHUNK, D)
        L = jnp.clip(jnp.cumsum(la_ch, axis=2), -20.0, 0.0)
        L_max = jnp.max(L, axis=2, keepdims=True)
        L_st = L - L_max
        cum_scaled = jnp.cumsum(jnp.exp(-L_st) * v_ch, axis=2)
        chunk_out = jnp.exp(L_st) * cum_scaled
        if nc > 1:
            bdecay = L[:, :, -1, :]
            bout = chunk_out[:, :, -1, :]
            cum_decay = jnp.clip(jnp.cumsum(bdecay, axis=1), -80.0, 0.0)
            stab = jnp.max(cum_decay, axis=1, keepdims=True)
            ncd = jnp.clip(cum_decay - stab, -20.0, 0.0)
            seeds = bout * jnp.exp(-ncd)
            shifted = jnp.pad(seeds[:, :-1], ((0, 0), (1, 0), (0, 0)))
            carries = jnp.cumsum(shifted, axis=1) * jnp.exp(ncd)
            final = chunk_out + carries[:, :, None, :] * jnp.exp(L)
        else:
            final = chunk_out
        final = final.astype(x.dtype).reshape(B, Np, D)[:, :N, :]
        v_mix = jnp.einsum('bnhd,hm->bnmd', final.reshape(B, N, H, d_head), head_mix)
        final = v_mix.reshape(B, N, D)
        out = final * gate @ out_proj_w
        return residual + out

    def _L0_xattn_ref(queries, keys, values, Wq, bq, Wk, bk, Wv, bv, Wo, bo):
        import jax, jax.numpy as jnp
        import numpy as np
        D_MODEL = 128
        N_HEADS = 16
        D_K = D_MODEL // N_HEADS
        B, L, _ = queries.shape
        H, E = (N_HEADS, D_K)
        Q = (queries @ Wq + bq).reshape(B, L, H, E).transpose(0, 2, 1, 3)
        K = (keys @ Wk + bk).reshape(B, L, H, E).transpose(0, 2, 1, 3)
        V = (values @ Wv + bv).reshape(B, L, H, E).transpose(0, 2, 1, 3)
        scores = jnp.einsum('bhqe,bhke->bhqk', Q, K) / jnp.sqrt(jnp.asarray(E, (scores_dtype := Q.dtype)))
        if L > 32:
            top_k = max(16, L // 4)
            top_vals, top_idx = jax.lax.top_k(scores, top_k)
            sparse = jnp.full_like(scores, -jnp.inf)
            bi = jnp.arange(B)[:, None, None, None]
            hi = jnp.arange(H)[None, :, None, None]
            qi = jnp.arange(L)[None, None, :, None]
            scores = sparse.at[bi, hi, qi, top_idx].set(top_vals)
        A = jax.nn.softmax(scores, axis=-1)
        context = jnp.einsum('bhqk,bhke->bhqe', A, V)
        context = context.transpose(0, 2, 1, 3).reshape(B, L, H * E)
        return context @ Wo + bo

    def _L0_ffn_ref(x, w1, b1, w2, b2):
        import jax, jax.numpy as jnp
        import numpy as np

        def fixed_quant(x, width, frac_width):
            scale = jnp.float32(2.0 ** frac_width)
            imax = jnp.float32(2 ** (width - 1) - 1)
            imin = jnp.float32(-2 ** (width - 1))
            return jnp.clip(jnp.round(x * scale), imin, imax) / scale
        IN_F, HID_F, OUT_F = (128, 512, 128)
        B, S = (4, 256)
        ACT_Q = (8, 4)
        W_Q = (8, 6)
        BIAS_Q = (8, 6)

        def quantized_linear(x, w, b):
            xq = fixed_quant(x, *ACT_Q)
            wq = fixed_quant(w, *W_Q)
            bq = fixed_quant(b, *BIAS_Q)
            return jnp.einsum('bsi,oi->bso', xq, wq) + bq

        def quantized_relu(x):
            return jax.nn.relu(fixed_quant(x, *ACT_Q))
        h = quantized_linear(x, w1, b1)
        h = quantized_relu(h)
        out = quantized_linear(h, w2, b2)
        return out
    x = _layernorm(x + _L0_attn_ref(x, L0_attn_norm_scale, L0_attn_conv_w, L0_attn_conv_b, L0_attn_in_proj_w, L0_attn_dt_bias, L0_attn_head_mix, L0_attn_out_proj_w), axis=-1)
    x = _layernorm(x + _L0_xattn_ref(x, ctx_1024, ctx_1024, L0_xattn_Wq, L0_xattn_bq, L0_xattn_Wk, L0_xattn_bk, L0_xattn_Wv, L0_xattn_bv, L0_xattn_Wo, L0_xattn_bo), axis=-1)
    x = _layernorm(x + _L0_ffn_ref(x, L0_ffn_w1, L0_ffn_b1, L0_ffn_w2, L0_ffn_b2), axis=-1)
    return x

_drawn_inputs = setup_inputs


def setup_inputs(seed=0):
    import zlib

    import numpy as np

    out = dict(_drawn_inputs(seed))
    spreads = {'L0_attn_norm_scale': (1.0, 0.6),
     'L0_xattn_bq': (0.0, 0.1),
     'L0_xattn_bk': (0.0, 0.8),
     'L0_xattn_bv': (0.0, 0.1),
     'L0_xattn_bo': (0.0, 0.1)}
    factors = {'L0_attn_conv_w': 4.176,
     'L0_attn_conv_b': 8.0,
     'L0_attn_in_proj_w': 4.106,
     'L0_attn_dt_bias': 4.792,
     'L0_attn_head_mix': 4.268,
     'L0_attn_out_proj_w': 4.096}
    for name, (base, spread) in spreads.items():
        noise = np.random.default_rng([zlib.crc32(name.encode()), seed]).standard_normal(out[name].shape)
        drawn = base * np.exp(spread * noise) if base else spread * noise
        out[name] = jnp.asarray(drawn.astype(out[name].dtype))
    for name, factor in factors.items():
        out[name] = (out[name] * factor).astype(out[name].dtype)
    return out
```

```python
from contextlib import ExitStack

import numpy as np

import concourse.bass as bass
from concourse import mybir

ALU = mybir.AluOpType
ACT = mybir.ActivationFunctionType
F32 = mybir.dt.float32
BF16 = mybir.dt.bfloat16

P = 128
NSEQ, S, D = 32, 128, 128
H = 16
DH = D // H
SB = 4
NBLK = NSEQ // SB
T = SB * S
HG = 4
NG = H // HG
UNITS = SB * NG
K = 4
CHUNK = 32
NCH = S // CHUNK
TOPK = max(16, S // 4)
ROUNDS = TOPK // 8
HID = 512
FC = HID // P
TAKEN = -3.0e38
SCALE = float(DH) ** -0.5
MAGIC = 1.5 * 2.0 ** 23
RMS_EPS, LN_EPS = 1e-6, 1e-5
EXP_FLOOR = -40.0
SP_CEIL = 30.0

C_ID, C_COS, C_SIN, C_HD, C_KM = 0, 128, 256, 384, 392
C_N = C_KM + NG


def constants():
    c = np.zeros((P, C_N), np.float32)
    c[:, C_ID:C_ID + P] = np.eye(P, dtype=np.float32)
    half = DH // 2
    inv = (1.0 / np.float32(10000.0) ** (np.arange(0, DH, 2, dtype=np.float32) / np.float32(DH))).astype(np.float32)
    freqs = np.arange(S, dtype=np.float32)[:, None] * inv[None, :]
    ch = np.arange(P)
    c[:, C_COS:C_COS + S] = np.cos(freqs).astype(np.float32).T[ch % half]
    sign = np.where(ch % DH < half, -1.0, 1.0).astype(np.float32)
    c[:, C_SIN:C_SIN + S] = np.sin(freqs).astype(np.float32).T[ch % half] * sign[:, None]
    c[ch, C_HD + ch % DH] = 1.0
    c[ch, C_KM + (ch // DH) % HG] = 1.0
    return c


class Steps:

    def __init__(self, eng, sem, held=None):
        self.eng, self.sem, self.held, self.n = eng, sem, held, 0

    def done(self, ins):
        ins.then_inc(self.sem, 1)
        self.n += 1
        return self.n

    def wait(self, n=None):
        self.eng.wait_ge(self.sem, self.n if n is None else n)

    def hold(self, sem, value):
        if isinstance(value, int) and value <= 0:
            return
        self.eng.wait_ge(sem, value)
        self.eng.nop().then_inc(self.held, 1)

    def restart(self):
        self.wait()
        self.eng.sem_clear(self.sem)
        self.n = 0


def wait(eng, sem, value):
    if isinstance(value, int) and value <= 0:
        return
    eng.wait_ge(sem, value)


def decoder_kernel(nc, x, ctx, norm_scale, conv_w, conv_b, in_proj_w, dt_bias, head_mix, out_proj_w,
                   Wq, bq, Wk, bk, Wv, bv, Wo, bo, w1, b1, w2, b2, const, out):
    with ExitStack() as es:
        def sb(name, shape, dt=F32):
            return es.enter_context(nc.sbuf_tensor(name, shape, dt))

        def bank(name):
            return es.enter_context(nc.psum_tensor(name, [P, T], F32))

        def sem(name):
            return es.enter_context(nc.semaphore(name))

        ps_scores, ps_probsT, ps_ctx = bank("ps_scores"), bank("ps_probsT"), bank("ps_ctx")
        ps_mixA, ps_mixB, ps_mixC = bank("ps_mixA"), bank("ps_mixB"), bank("ps_mixC")
        ps_ffnA, ps_ffnB = bank("ps_ffnA"), bank("ps_ffnB")
        ps_ffnA16 = ps_ffnA[:, :].bitcast(BF16)
        ps_ffnB16 = ps_ffnB[:, :].bitcast(BF16)

        cst = sb("cst", [P, C_N])
        ident = cst[:, C_ID:C_ID + P]
        ident16 = sb("ident16", [P, P], BF16)
        wq_sb, wk_sb, wv_sb, wo_sb = (sb(n, [P, D]) for n in ("wq_sb", "wk_sb", "wv_sb", "wo_sb"))
        win_sb = sb("win_sb", [P, 3 * D])
        wvswap = sb("wvswap", [P, H, DH])
        wout_sb = sb("wout_sb", [P, D])
        nscale, convb, dtb = sb("nscale", [P, 1]), sb("convb", [P, 1]), sb("dtb", [P, 1])
        bq_sb, bk_sb, bv_sb = sb("bq_sb", [P, 1]), sb("bk_sb", [P, 1]), sb("bv_sb", [P, 1])
        convw = sb("convw", [P, K])
        convdiag = sb("convdiag", [P, K, P])
        mixrep = sb("mixrep", [P, H])
        mixkron = sb("mixkron", [P, H, DH])
        bkmask = sb("bkmask", [P, HG])
        bo_rep = sb("bo_rep", [P, D])
        w1_sb, w1_t, w1_u = sb("w1_sb", [P, FC, P]), sb("w1_t", [P, FC, P]), sb("w1_u", [P, FC, P])
        w2_sb, w2_t, w2_u = sb("w2_sb", [P, HID]), sb("w2_t", [P, HID]), sb("w2_u", [P, HID])
        w1q, w2q = sb("w1q", [P, FC, P], BF16), sb("w2q", [P, HID], BF16)
        w1T, w2T = sb("w1T", [P, FC, P], BF16), sb("w2T", [P, FC, P], BF16)
        b1_sb, b1_t, b1_u, b1_s = (sb(n, [P, FC]) for n in ("b1_sb", "b1_t", "b1_u", "b1_s"))
        b2_sb, b2_t, b2_u = (sb(n, [1, D]) for n in ("b2_sb", "b2_t", "b2_u"))
        b2q = sb("b2q", [1, D], BF16)
        ones_row = sb("ones_row", [1, P], BF16)
        keep = sb("keep", [P, T])
        keepc = sb("keepc", [P, SB * NCH])
        neghalf = sb("neghalf", [P, SB])

        x_sb = sb("x_sb", [P, SB, D])
        sqjunk, ss = sb("sqjunk", [P, SB, D]), sb("ss", [P, SB])
        ms, rms = sb("ms", [P, SB]), sb("rms", [P, SB])
        xs, xnr = sb("xs", [P, SB, D]), sb("xnr", [P, T])
        xnp = sb("xnp", [P, SB, K - 1 + S])
        zc, ze, zl, zs, xc = (sb(n, [P, T]) for n in ("zc", "ze", "zl", "zs", "xc"))
        v_sb, vw_sb, ra, rb, vrot, vin = (sb(n, [P, T]) for n in ("v_sb", "vw_sb", "ra", "rb", "vrot", "vin"))
        dtc, dte, dts, dt_ = (sb(n, [P, T]) for n in ("dtc", "dte", "dts", "dt_"))
        gc, ge, gl, gate = (sb(n, [P, T]) for n in ("gc", "ge", "gl", "gate"))
        cum, cc, dst = (sb(n, [P, T]) for n in ("cum", "cc", "dst"))
        egrow, edecay, ecar = (sb(n, [P, T]) for n in ("egrow", "edecay", "ecar"))
        w_, cs, co, ce, fin = (sb(n, [P, T]) for n in ("w_", "cs", "co", "ce", "fin"))
        cdr, cd, cm, cn, eM, enM, seeds, cse, carr = (
            sb(n, [P, SB * NCH]) for n in ("cdr", "cd", "cm", "cn", "eM", "enM", "seeds", "cse", "carr"))
        mx, y = sb("mx", [P, T]), sb("y", [P, T])
        x1p, x1 = sb("x1p", [P, SB, D]), sb("x1", [P, SB, D])
        x1T = sb("x1T", [P, T])
        ctx_sb, ctxT = sb("ctx_sb", [P, SB, D]), sb("ctxT", [P, T])

        qT = sb("qT", [P, T])
        kmaskT = sb("kmaskT", [P, SB, HG, S])
        vaug = sb("vaug", [P, SB, H, DH + 1])
        sc_sb = sb("sc_sb", [P, 4, HG, S])
        rest = sb("rest", [P, 4, HG, S])
        top = sb("top", [P, 4, HG, TOPK])
        negmax = sb("negmax", [P, 4, HG])
        ex = sb("ex", [P, 2, HG, S])
        msk = sb("msk", [P, 2, HG, S])
        pr = sb("pr", [P, 2, HG, S])
        prT = sb("prT", [P, 2, HG, S])
        ctxo = sb("ctxo", [P, 2, H, DH + 1])
        rden = sb("rden", [P, 2, H])
        on = sb("on", [P, SB, H, DH])

        oT = sb("oT", [P, T])
        x1h, x2p, x2, x3p, out_sb = (sb(n, [P, SB, D]) for n in ("x1h", "x2p", "x2", "x3p", "out_sb"))
        q1, q2 = sb("q1", [P, SB, D]), sb("q2", [P, SB, D])
        xq, xqT = sb("xq", [P, SB, D], BF16), sb("xqT", [P, T], BF16)
        hr, hm = sb("hr", [P, FC, T]), sb("hm", [P, FC, T])
        hq = sb("hq", [P, FC, T], BF16)
        bst = [sb(f"bst{n}", [P, SB, 6]) for n in range(3)]
        mv = [sb(f"mv{n}", [P, SB, 2]) for n in range(3)]
        ve = [sb(f"ve{n}", [P, SB]) for n in range(3)]
        rs = [sb(f"rs{n}", [P, SB]) for n in range(3)]
        nm = [sb(f"nm{n}", [P, SB]) for n in range(3)]
        nb = [sb(f"nb{n}", [P, SB]) for n in range(3)]

        names = """x_loaded ctx_loaded w_loaded wl_loaded f_loaded out_stored out_free
            setup_pool ffn_quant ffn_wT ffn_w
            ss_ready xs_ready xsT_ready xnr_ready xn_ready conv_ready zc_ready sig_ready xc_ready
            dtraw_ready vraw_ready v_copied dtc_ready graw_ready gc_ready softplus_ready dt_ready
            gate_ready cum_ready cc_ready dst_ready egrow_ready edecay_ready w_ready cdr_ready
            cn_ready em_ready cs_ready seeds_ready cse_ready fin_ready mix_ready mx_ready y_ready
            outp_ready stats1_ready ln1_ready x1_ready x1T_ready x1T_copied qraw_ready q_ready
            ctxT_ready ctxT_copied kraw_ready k_ready vps_ready v_ready
            scores_ready scores_copied topk_done negmax_ready exps_ready probs_ready
            probsT_ready probsT_copied pv_done ctx_copied rden_ready on_ready
            onT_ready oT_copied attn_ready x1h_ready stats2_ready ln2_ready x2_ready xq_ready
            xqT_ready xqT_copied h_ready relu_ready hm_ready hq_ready out2_ready
            stats3_ready ln3_ready out_ready
            pool_steps dve_steps act_steps pool_held dve_held""".split()
        q = {n: sem(n) for n in names}

        x_v = x.rearrange("(k b) s d -> k s b d", b=SB)
        ctx_v = ctx.rearrange("(k b) s d -> k s b d", b=SB)
        out_v = out.rearrange("(k b) s d -> k s b d", b=SB)

        def col(v):
            return v.rearrange("(p o) -> p o", o=1)

        def seqs(t):
            return t.rearrange("p (b s) -> p b s", b=SB)

        def chunks(t):
            return t.rearrange("p (c s) -> p c s", s=CHUNK)

        W_LOADS, WL_LOADS, F_LOADS = 6, 10, 4
        block = es.enter_context(nc.Block())

        @block.sync
        def _(sp):
            def load_x(k):
                if not (isinstance(k, int) and k == 0):
                    sp.wait_ge(q["stats1_ready"], k)
                sp.dma_start(x_sb[:, :, :], x_v[k]).then_inc(q["x_loaded"], 16)

            def load_ctx(k):
                if not (isinstance(k, int) and k == 0):
                    sp.wait_ge(q["ctxT_ready"], k)
                sp.dma_start(ctx_sb[:, :, :], ctx_v[k]).then_inc(q["ctx_loaded"], 16)

            def store(k):
                sp.wait_ge(q["out_ready"], k + 1)
                sp.dma_start(out_v[k], out_sb[:, :, :]).then_inc(q["out_free"], 16)

            load_x(0)
            sp.dma_start(cst[:, :], const[:, :]).then_inc(q["w_loaded"], 16)
            sp.dma_start(nscale[:, :], col(norm_scale)).then_inc(q["w_loaded"], 16)
            sp.dma_start(convw[:, :], conv_w.rearrange("d o k -> d (o k)")).then_inc(q["w_loaded"], 16)
            sp.dma_start(convb[:, :], col(conv_b)).then_inc(q["w_loaded"], 16)
            sp.dma_start(win_sb[:, :], in_proj_w[:, :]).then_inc(q["w_loaded"], 16)
            sp.dma_start(dtb[:, :], col(dt_bias)).then_inc(q["w_loaded"], 16)
            load_ctx(0)
            sp.nop().then_inc(q["out_free"], 16)
            load_x(1)
            load_ctx(1)
            load_x(2)
            load_ctx(2)
            with sp.Fori(1, NBLK - 2) as i:
                load_x(i + 2)
                load_ctx(i + 2)
                store(i - 1)
            for k in range(NBLK - 3, NBLK):
                store(k)
            sp.wait_ge(q["out_free"], 16 * (NBLK + 1))

        @block.gpsimd
        def _(g):
            st = Steps(g, q["pool_steps"], q["pool_held"])

            def setup():
                st.done(g.memset(keep[:, :], 1.0))
                st.done(g.memset(keepc[:, :], 1.0))
                st.done(g.memset(neghalf[:, :], -0.5))
                st.done(g.memset(ones_row[:, :], 1.0))
                st.done(g.memset(xnp[:, :, 0:K - 1], 0.0))
                st.done(g.memset(carr[:, :], 0.0))
                st.done(g.memset(vaug[:, :, :, DH:DH + 1], 1.0))
                st.wait()
                st.done(g.memset(chunks(keep[:, :])[:, :, 0:1], 0.0))
                st.done(g.memset(keepc.rearrange("p (b c) -> p b c", b=SB)[:, :, 0:1], 0.0))

            def setup_weights():
                g.wait_ge(q["w_loaded"], 16 * W_LOADS)
                g.wait_ge(q["wl_loaded"], 16 * WL_LOADS)
                for k in range(K):
                    st.done(g.tensor_scalar(convdiag[:, k, :], ident, convw[:, k:k + 1], None, ALU.mult))
                wv = win_sb[:, D:2 * D].rearrange("p (h d) -> p h d", h=H)
                st.done(g.tensor_copy(wvswap[:, :, 0:DH // 2], wv[:, :, DH // 2:DH]))
                st.done(g.tensor_copy(wvswap[:, :, DH // 2:DH], wv[:, :, 0:DH // 2]))
                st.done(g.tensor_tensor(mixkron[:, :, :], mixrep[:, :].unsqueeze(2).broadcast_to([P, H, DH]),
                                        cst[:, C_HD:C_HD + DH].unsqueeze(1).broadcast_to([P, H, DH]), ALU.mult))
                st.done(g.tensor_scalar(bkmask[:, :], cst[:, C_KM:C_KM + HG], bk_sb[:, :], None, ALU.mult))
                st.done(g.tensor_copy(ident16[:, :], ident))
                st.wait()
                g.nop().then_inc(q["setup_pool"], 1)

            def layernorm(n, stats, ready, k):
                st.hold(q[stats], k + 1)
                st.done(g.tensor_scalar(ve[n][:, :], mv[n][:, :, 1], LN_EPS, None, ALU.add))
                st.wait()
                st.done(g.tensor_tensor(rs[n][:, :], ve[n][:, :], neghalf[:, :], ALU.pow))
                st.wait()
                st.done(g.tensor_tensor(nm[n][:, :], mv[n][:, :, 0], rs[n][:, :], ALU.mult))
                st.wait()
                g.tensor_scalar(nb[n][:, :], nm[n][:, :], -1.0, None, ALU.mult).then_inc(q[ready], 1)

            def rms_scale(k):
                st.hold(q["ss_ready"], k + 1)
                st.done(g.tensor_scalar(ms[:, :], ss[:, :], 1.0 / D, RMS_EPS, ALU.mult, ALU.add))
                st.wait()
                st.done(g.tensor_tensor(rms[:, :], ms[:, :], neghalf[:, :], ALU.pow))
                st.wait()
                g.tensor_tensor(xs[:, :, :], x_sb[:, :, :], rms[:, :].unsqueeze(2).broadcast_to([P, SB, D]),
                                ALU.mult).then_inc(q["xs_ready"], 1)

            def clip_xn(k):
                st.hold(q["xnr_ready"], k + 1)
                g.tensor_scalar(xnp[:, :, K - 1:], seqs(xnr), 60000.0, -60000.0, ALU.min, ALU.max)\
                    .then_inc(q["xn_ready"], 1)

            def silu(k):
                g.wait_ge(q["sig_ready"], k + 1)
                g.tensor_tensor(xc[:, :], zc[:, :], zs[:, :], ALU.mult).then_inc(q["xc_ready"], 1)

            def rope(k):
                g.wait_ge(q["v_copied"], k + 1)
                st.done(g.tensor_tensor(seqs(ra), seqs(v_sb),
                                        cst[:, C_COS:C_COS + S].unsqueeze(1).broadcast_to([P, SB, S]), ALU.mult))
                st.done(g.tensor_tensor(seqs(rb), seqs(vw_sb),
                                        cst[:, C_SIN:C_SIN + S].unsqueeze(1).broadcast_to([P, SB, S]), ALU.mult))
                st.wait()
                st.done(g.tensor_tensor(vrot[:, :], ra[:, :], rb[:, :], ALU.add))

            def clip_dt(k):
                st.hold(q["softplus_ready"], k + 1)
                g.tensor_scalar(dt_[:, :], dts[:, :], 2.0, 0.001, ALU.min, ALU.max).then_inc(q["dt_ready"], 1)
                st.wait()
                g.wait_ge(q["dt_ready"], k + 1)
                st.done(g.tensor_tensor(vin[:, :], vrot[:, :], dt_[:, :], ALU.mult))

            def decay(k):
                st.hold(q["cum_ready"], k + 1)
                g.tensor_scalar(cc[:, :], cum[:, :], 20.0, 0.0, ALU.min, ALU.max).then_inc(q["cc_ready"], 1)
                g.wait_ge(q["cc_ready"], k + 1)
                g.tensor_tensor(chunks(dst), chunks(cc),
                                chunks(cc)[:, :, 0:1].broadcast_to([P, SB * NCH, CHUNK]), ALU.subtract)\
                    .then_inc(q["dst_ready"], 1)

            def grow(k):
                st.wait()
                g.wait_ge(q["egrow_ready"], k + 1)
                g.tensor_tensor(w_[:, :], egrow[:, :], vin[:, :], ALU.mult).then_inc(q["w_ready"], 1)

            def chunk_decay(k):
                st.hold(q["cdr_ready"], k + 1)
                st.done(g.tensor_scalar(cd[:, :], cdr[:, :], 80.0, 0.0, ALU.min, ALU.max))
                st.wait()
                cdv = cd.rearrange("p (b c) -> p b c", b=SB)
                st.done(g.tensor_tensor(cm.rearrange("p (b c) -> p b c", b=SB), cdv,
                                        cdv[:, :, 0:1].broadcast_to([P, SB, NCH]), ALU.subtract))
                st.wait()
                g.tensor_scalar(cn[:, :], cm[:, :], 20.0, 0.0, ALU.min, ALU.max).then_inc(q["cn_ready"], 1)

            def chunk_out(k):
                g.wait_ge(q["edecay_ready"], k + 1)
                g.wait_ge(q["cs_ready"], k + 1)
                n = st.done(g.tensor_tensor(co[:, :], edecay[:, :], cs[:, :], ALU.mult))
                g.wait_ge(q["em_ready"], k + 1)
                st.wait(n)
                g.tensor_tensor(seeds[:, :], chunks(co)[:, :, CHUNK - 1], eM[:, :], ALU.mult)\
                    .then_inc(q["seeds_ready"], 1)

            def carry(k):
                g.wait_ge(q["cse_ready"], k + 1)
                cv, sv, ev = (t.rearrange("p (b c) -> p b c", b=SB) for t in (carr, cse, enM))
                st.done(g.tensor_tensor(cv[:, :, 1:NCH], sv[:, :, 0:NCH - 1], ev[:, :, 1:NCH], ALU.mult))
                st.wait()
                st.done(g.tensor_tensor(chunks(ce), chunks(ecar),
                                        carr[:, :].unsqueeze(2).broadcast_to([P, SB * NCH, CHUNK]), ALU.mult))
                st.wait()
                g.tensor_tensor(fin[:, :], co[:, :], ce[:, :], ALU.add).then_inc(q["fin_ready"], 1)

            def gated(k):
                g.wait_ge(q["gate_ready"], k + 1)
                g.wait_ge(q["mx_ready"], k + 1)
                g.tensor_tensor(y[:, :], mx[:, :], gate[:, :], ALU.mult).then_inc(q["y_ready"], 1)

            def neg_max(n, r):
                st.hold(q["topk_done"], n + 1)
                g.tensor_scalar(negmax[:, r, :], top[:, r, :, 0], -SCALE, None, ALU.mult)\
                    .then_inc(q["negmax_ready"], 1)

            def mask(n, r):
                return st.done(g.tensor_scalar(msk[:, r % 2, :, :], rest[:, r, :, :], TAKEN, None, ALU.is_le))

            def probs(n, r, masked):
                wait(g, q["probsT_ready"], n - 1)
                g.wait_ge(q["exps_ready"], n + 1)
                st.wait(masked)
                g.tensor_tensor(pr[:, r % 2, :, :], ex[:, r % 2, :, :], msk[:, r % 2, :, :], ALU.mult)\
                    .then_inc(q["probs_ready"], 1)

            def normalise(k, b):
                g.wait_ge(q["rden_ready"], SB * k + b + 1)
                if b == 0:
                    wait(g, q["onT_ready"], k)
                g.tensor_tensor(on[:, b, :, :], ctxo[:, b % 2, :, 0:DH],
                                rden[:, b % 2, :].unsqueeze(2).broadcast_to([P, H, DH]), ALU.mult)\
                    .then_inc(q["on_ready"], 1)

            def residual(k):
                g.wait_ge(q["x1_ready"], k + 1)
                wait(g, q["stats2_ready"], k)
                g.tensor_tensor(x1h[:, :, :], x1[:, :, :], bo_rep[:, :].unsqueeze(1).broadcast_to([P, SB, D]),
                                ALU.add).then_inc(q["x1h_ready"], 1)

            def quantise(k):
                st.hold(q["x2_ready"], k + 1)
                st.done(g.tensor_scalar(q1[:, :, :], x2[:, :, :], 16.0, 127.0, ALU.mult, ALU.min))
                st.wait()
                st.done(g.tensor_scalar(q2[:, :, :], q1[:, :, :], -128.0, MAGIC, ALU.max, ALU.add))
                st.wait()
                g.tensor_scalar(xq[:, :, :], q2[:, :, :], -MAGIC, None, ALU.add).then_inc(q["xq_ready"], 1)

            def hidden(k, c):
                st.hold(q["relu_ready"], FC * k + c + 1)
                g.tensor_scalar(hm[:, c, :], hr[:, c, :], 127.0, MAGIC, ALU.min, ALU.add).then_inc(q["hm_ready"], 1)

            def body(i, first, last):
                mixer, ffn = not last, not first
                masked = None
                for p in range(2 * UNITS):
                    u, odd = divmod(p, 2)
                    n, r = UNITS * i + u - 1, (u - 1) % 4
                    if not (first and u < 1):
                        if not odd:
                            neg_max(n, r)
                            masked = mask(n, r)
                        else:
                            probs(n, r, masked)
                    if not odd and u % 4 == 3 and not (first and u == 3):
                        pass
                    if odd == 0 and u % 4 == 3:
                        b = (u - 7) // 4
                        if b >= 0:
                            normalise(i, b)
                        elif not first:
                            normalise(i - 1, SB - 1)
                    if mixer:
                        mixer_at(i + 1, p)
                    if ffn:
                        ffn_at(i - 1, p)
                    if p == 16:
                        residual(i)
                st.restart()

            def mixer_at(k, p):
                if p == 0:
                    rms_scale(k)
                if p == 1:
                    clip_xn(k)
                if p == 5:
                    silu(k)
                if p == 7:
                    rope(k)
                if p == 8:
                    clip_dt(k)
                if p == 10:
                    decay(k)
                if p == 11:
                    grow(k)
                if p == 12:
                    chunk_decay(k)
                if p == 13:
                    chunk_out(k)
                if p == 15:
                    carry(k)
                if p == 17:
                    gated(k)
                if p == 20:
                    layernorm(0, "stats1_ready", "ln1_ready", k)

            def ffn_at(k, p):
                if p == 12:
                    layernorm(1, "stats2_ready", "ln2_ready", k)
                if p == 13:
                    quantise(k)
                if p in (17, 18):
                    hidden(k, p - 17)
                if p in (20, 21):
                    hidden(k, p - 18)
                if p == 24:
                    layernorm(2, "stats3_ready", "ln3_ready", k)

            setup()
            rms_scale(0)
            setup_weights()
            for p in range(1, 2 * UNITS):
                mixer_at(0, p)
            st.restart()
            body(0, True, False)
            with g.Fori(1, NBLK - 1) as i:
                body(i, False, False)
            body(NBLK - 1, False, True)
            n = UNITS * NBLK - 1
            neg_max(n, 3)
            probs(n, 3, mask(n, 3))
            normalise(NBLK - 1, SB - 1)
            for p in range(2 * UNITS):
                ffn_at(NBLK - 1, p)

        @block.vector
        def _(v):
            st = Steps(v, q["dve_steps"], q["dve_held"])

            def top_rounds(n, r, rounds):
                if 0 in rounds:
                    wait_n = n + 1
                    st.hold(q["scores_copied"], wait_n)
                    st.hold(q["probs_ready"], n - 3)
                for rd in rounds:
                    base = st.n
                    for j in range(HG):
                        src = sc_sb[:, r, j, :] if rd == 0 else rest[:, r, j, :]
                        if rd > 0:
                            st.wait(mr[j])
                        mx8[j] = st.done(v.max(top[:, r, j, 8 * rd:8 * rd + 8], src))
                    for j in range(HG):
                        src = sc_sb[:, r, j, :] if rd == 0 else rest[:, r, j, :]
                        st.wait(mx8[j])
                        ins = v.match_replace(rest[:, r, j, :], top[:, r, j, 8 * rd:8 * rd + 8], src, TAKEN)
                        if rd == ROUNDS - 1 and j == HG - 1:
                            ins.then_inc(q["topk_done"], 1)
                        else:
                            mr[j] = st.done(ins)

            mr, mx8 = [0] * HG, [0] * HG

            def moments(n, src, ready):
                st.wait()
                for b in range(SB):
                    first = st.done(v.bn_stats(bst[n][:, b, :], src[:, b, :]))
                for b in range(SB):
                    st.wait(first - SB + 1 + b)
                    ins = v.bn_aggr(mv[n][:, b, :], bst[n][:, b, :])
                    if b < SB - 1:
                        st.done(ins)
                ins.then_inc(q[ready], 1)

            def conv_clamp(k):
                v.wait_ge(q["conv_ready"], k + 1)
                v.tensor_scalar(zc[:, :], ps_mixB[:, :], convb[:, :], EXP_FLOOR, ALU.add, ALU.max)\
                    .then_inc(q["zc_ready"], 1)

            def dt_clamp(k):
                v.wait_ge(q["dtraw_ready"], k + 1)
                v.tensor_scalar(dtc[:, :], ps_mixA[:, :], dtb[:, :], SP_CEIL, ALU.add, ALU.min)\
                    .then_inc(q["dtc_ready"], 1)

            def gate_clamp(k):
                v.wait_ge(q["graw_ready"], k + 1)
                v.tensor_scalar(gc[:, :], ps_mixB[:, :], EXP_FLOOR, None, ALU.max).then_inc(q["gc_ready"], 1)

            def scan(ready, out_, keep_, in_, sem_, k):
                v.wait_ge(q[ready], k + 1)
                v.tensor_tensor_scan(out_, keep_, in_, 0.0, ALU.mult, ALU.add).then_inc(q[sem_], 1)

            def x1_pre(k):
                v.wait_ge(q["outp_ready"], k + 1)
                st.done(v.scalar_tensor_tensor(out=x1p[:, :, :], in0=x_sb[:, :, :], scalar=2.0,
                                               in1=seqs(ps_mixC), op0=ALU.mult, op1=ALU.add))
                moments(0, x1p, "stats1_ready")

            def recip(k, b):
                v.wait_ge(q["ctx_copied"], SB * k + b + 1)
                v.reciprocal(rden[:, b % 2, :], ctxo[:, b % 2, :, DH]).then_inc(q["rden_ready"], 1)

            def x2_pre(k):
                v.wait_ge(q["x1h_ready"], k + 1)
                v.wait_ge(q["attn_ready"], k + 1)
                st.done(v.tensor_tensor(x2p[:, :, :], seqs(ps_ffnB), x1h[:, :, :], ALU.add))
                moments(1, x2p, "stats2_ready")

            def x3_pre(k):
                v.wait_ge(q["out2_ready"], k + 1)
                st.done(v.scalar_tensor_tensor(out=x3p[:, :, :], in0=seqs(ps_ffnA), scalar=2.0 ** -10,
                                               in1=x2[:, :, :], op0=ALU.mult, op1=ALU.add))
                moments(2, x3p, "stats3_ready")

            def mixer_at(k, p):
                if p == 3:
                    conv_clamp(k)
                if p == 7:
                    dt_clamp(k)
                if p == 8:
                    gate_clamp(k)
                if p == 9:
                    scan("dt_ready", cum[:, :], keep[:, :], dt_[:, :], "cum_ready", k)
                if p == 11:
                    scan("cc_ready", cdr[:, :], keepc[:, :], chunks(cc)[:, :, CHUNK - 1], "cdr_ready", k)
                if p == 13:
                    scan("w_ready", cs[:, :], keep[:, :], w_[:, :], "cs_ready", k)
                if p == 15:
                    scan("seeds_ready", cse[:, :], keepc[:, :], seeds[:, :], "cse_ready", k)
                if p == 19:
                    x1_pre(k)

            def ffn_at(k, p):
                if p == 11:
                    x2_pre(k)
                if p == 23:
                    x3_pre(k)

            def body(i, first, last):
                for p in range(2 * UNITS):
                    u, odd = divmod(p, 2)
                    if not odd and u % 4 == 3:
                        b = (u - 7) // 4
                        if b >= 0:
                            recip(i, b)
                        elif not first:
                            recip(i - 1, SB - 1)
                    if not last:
                        mixer_at(i + 1, p)
                    if not first:
                        ffn_at(i - 1, p)
                    half = ROUNDS // 2
                    top_rounds(UNITS * i + u, u % 4, range(half, ROUNDS) if odd else range(half))
                st.restart()

            def quantise_weight(src, t, u, out_, factor=1.0):
                st.done(v.tensor_scalar(t, src, 64.0, 127.0, ALU.mult, ALU.min))
                st.wait()
                st.done(v.tensor_scalar(u, t, -128.0, MAGIC, ALU.max, ALU.add))
                st.wait()
                st.done(v.tensor_scalar(out_, u, -MAGIC, factor, ALU.add, ALU.mult))

            v.wait_ge(q["f_loaded"], 16 * F_LOADS)
            quantise_weight(w1_sb[:, :, :], w1_t[:, :, :], w1_u[:, :, :], w1q[:, :, :])
            quantise_weight(w2_sb[:, :], w2_t[:, :], w2_u[:, :], w2q[:, :])
            quantise_weight(b1_sb[:, :], b1_t[:, :], b1_u[:, :], b1_s[:, :], 0.25)
            quantise_weight(b2_sb[:, :], b2_t[:, :], b2_u[:, :], b2q[:, :], 16.0)
            st.wait()
            v.nop().then_inc(q["ffn_quant"], 1)
            for p in range(2 * UNITS):
                if p == 3:
                    v.wait_ge(q["setup_pool"], 1)
                mixer_at(0, p)
            st.restart()
            body(0, True, False)
            with v.Fori(1, NBLK - 1) as i:
                body(i, False, False)
            body(NBLK - 1, False, True)
            recip(NBLK - 1, SB - 1)
            for p in range(2 * UNITS):
                ffn_at(NBLK - 1, p)

        @block.scalar
        def _(a):
            st = Steps(a, q["act_steps"])

            def copy(out_, in_, bias=0.0, scale=1.0):
                return a.activation(out_, in_, ACT.Identity, bias=bias, scale=scale)

            def sigmoid(src, e, l, out_, ready):
                st.done(a.activation(e, src, ACT.Exp, scale=-1.0))
                st.wait()
                st.done(a.activation(l, e, ACT.Ln, bias=1.0))
                st.wait()
                a.activation(out_, l, ACT.Exp, scale=-1.0).then_inc(q[ready], 1)

            def apply_norm(n, src, out_, ready):
                for b in range(SB):
                    ins = copy(out_[:, b, :], src[:, b, :], bias=nb[n][:, b:b + 1], scale=rs[n][:, b:b + 1])
                ins.then_inc(q[ready], 1)

            def squares(k):
                a.wait_ge(q["x_loaded"], 16 * (k + 1))
                for b in range(SB):
                    ins = a.activation(sqjunk[:, b, :], x_sb[:, b, :], ACT.Square, accum_out=ss[:, b:b + 1])
                ins.then_inc(q["ss_ready"], 1)

            def xn_copy(k):
                a.wait_ge(q["xsT_ready"], k + 1)
                copy(xnr[:, :], ps_mixA[:, :], scale=nscale[:, :]).then_inc(q["xnr_ready"], 1)

            def conv_sigmoid(k):
                a.wait_ge(q["zc_ready"], k + 1)
                sigmoid(zc[:, :], ze[:, :], zl[:, :], zs[:, :], "sig_ready")

            def v_copy(k):
                a.wait_ge(q["vraw_ready"], k + 1)
                copy(v_sb[:, :], ps_mixB[:, :])
                copy(vw_sb[:, :], ps_mixC[:, :]).then_inc(q["v_copied"], 1)

            def softplus(k):
                a.wait_ge(q["dtc_ready"], k + 1)
                st.done(a.activation(dte[:, :], dtc[:, :], ACT.Exp))
                st.wait()
                a.activation(dts[:, :], dte[:, :], ACT.Ln, bias=1.0).then_inc(q["softplus_ready"], 1)

            def gate_sigmoid(k):
                a.wait_ge(q["gc_ready"], k + 1)
                sigmoid(gc[:, :], ge[:, :], gl[:, :], gate[:, :], "gate_ready")

            def decays(k):
                a.wait_ge(q["dst_ready"], k + 1)
                a.activation(egrow[:, :], dst[:, :], ACT.Exp).then_inc(q["egrow_ready"], 1)
                a.activation(edecay[:, :], dst[:, :], ACT.Exp, scale=-1.0).then_inc(q["edecay_ready"], 1)
                st.done(a.activation(ecar[:, :], cc[:, :], ACT.Exp, scale=-1.0))

            def chunk_exps(k):
                a.wait_ge(q["cn_ready"], k + 1)
                st.done(a.activation(eM[:, :], cn[:, :], ACT.Exp))
                st.done(a.activation(enM[:, :], cn[:, :], ACT.Exp, scale=-1.0))
                st.wait()
                a.nop().then_inc(q["em_ready"], 1)

            def mx_copy(k):
                a.wait_ge(q["mix_ready"], k + 1)
                copy(mx[:, :], ps_mixA[:, :]).then_inc(q["mx_ready"], 1)

            def x1_apply(k):
                wait(a, q["x1h_ready"], k)
                a.wait_ge(q["ln1_ready"], k + 1)
                apply_norm(0, x1p, x1, "x1_ready")

            def x1T_copy(k):
                a.wait_ge(q["x1T_ready"], k + 1)
                copy(x1T[:, :], ps_mixA[:, :]).then_inc(q["x1T_copied"], 1)

            def ctxT_copy(k):
                wait(a, q["vps_ready"], k)
                a.wait_ge(q["ctxT_ready"], k + 1)
                copy(ctxT[:, :], ps_mixC[:, :]).then_inc(q["ctxT_copied"], 1)

            def q_copy(k):
                wait(a, q["scores_ready"], UNITS * k)
                a.wait_ge(q["qraw_ready"], k + 1)
                copy(qT[:, :], ps_mixA[:, :], bias=bq_sb[:, :]).then_inc(q["q_ready"], 1)

            def k_copy(k):
                a.wait_ge(q["kraw_ready"], k + 1)
                for j in range(HG):
                    ins = copy(kmaskT[:, :, j, :], seqs(ps_mixB), bias=bkmask[:, j:j + 1],
                               scale=cst[:, C_KM + j:C_KM + j + 1])
                ins.then_inc(q["k_ready"], 1)

            def v_attn_copy(k):
                wait(a, q["pv_done"], UNITS * k)
                a.wait_ge(q["vps_ready"], k + 1)
                copy(vaug[:, :, :, 0:DH], ps_ffnA.rearrange("p (b h d) -> p b h d", b=SB, h=H))\
                    .then_inc(q["v_ready"], 1)

            def scores_copy(n, r):
                wait(a, q["exps_ready"], n - 3)
                a.wait_ge(q["scores_ready"], n + 1)
                copy(sc_sb[:, r, :, :], ps_scores.rearrange("p (j s) -> p j s", j=HG))\
                    .then_inc(q["scores_copied"], 1)

            def exps(n, r):
                wait(a, q["probs_ready"], n - 1)
                a.wait_ge(q["negmax_ready"], n + 1)
                for j in range(HG):
                    ins = a.activation(ex[:, r % 2, j, :], sc_sb[:, r, j, :], ACT.Exp,
                                       bias=negmax[:, r, j:j + 1], scale=SCALE)
                ins.then_inc(q["exps_ready"], 1)

            def probsT_copy(n, r):
                wait(a, q["pv_done"], n - 1)
                a.wait_ge(q["probsT_ready"], n + 1)
                copy(prT[:, r % 2, :, :], ps_probsT.rearrange("p (j s) -> p j s", j=HG))\
                    .then_inc(q["probsT_copied"], 1)

            def ctx_copy(k, b):
                wait(a, q["on_ready"], SB * k + b - 1)
                a.wait_ge(q["pv_done"], UNITS * k + NG * (b + 1))
                copy(ctxo[:, b % 2, :, :], ps_ctx[:, 0:H * (DH + 1)].rearrange("p (h d) -> p h d", h=H))\
                    .then_inc(q["ctx_copied"], 1)

            def oT_copy(k):
                a.wait_ge(q["onT_ready"], k + 1)
                copy(oT[:, :], ps_ffnA[:, :], bias=bv_sb[:, :]).then_inc(q["oT_copied"], 1)

            def x2_apply(k):
                a.wait_ge(q["ln2_ready"], k + 1)
                apply_norm(1, x2p, x2, "x2_ready")

            def xqT_copy(k):
                a.wait_ge(q["xqT_ready"], k + 1)
                copy(xqT[:, :], ps_ffnA16[:, 0:T]).then_inc(q["xqT_copied"], 1)

            def relu(k, c):
                a.wait_ge(q["h_ready"], FC * k + c + 1)
                a.activation(hr[:, c, :], (ps_ffnB if c % 2 == 0 else ps_ffnA)[:, :], ACT.Relu,
                             bias=b1_s[:, c:c + 1], scale=1.0 / 64).then_inc(q["relu_ready"], 1)

            def h_round(k, c):
                a.wait_ge(q["hm_ready"], FC * k + c + 1)
                copy(hq[:, c, :], hm[:, c, :], bias=-MAGIC).then_inc(q["hq_ready"], 1)

            def out_apply(k):
                a.wait_ge(q["out_free"], 16 * (k + 1))
                a.wait_ge(q["ln3_ready"], k + 1)
                apply_norm(2, x3p, out_sb, "out_ready")

            def mixer_at(k, p):
                if p == 0:
                    squares(k)
                if p == 1:
                    xn_copy(k)
                if p == 4:
                    conv_sigmoid(k)
                if p == 6:
                    v_copy(k)
                if p == 7:
                    softplus(k)
                if p == 9:
                    gate_sigmoid(k)
                if p == 10:
                    decays(k)
                if p == 12:
                    chunk_exps(k)
                if p == 17:
                    mx_copy(k)
                if p == 20:
                    x1_apply(k)
                if p == 21:
                    x1T_copy(k)
                if p == 23:
                    ctxT_copy(k)
                if p == 28:
                    q_copy(k)
                    k_copy(k)

            def ffn_at(k, p):
                if p == 8:
                    oT_copy(k)
                if p == 12:
                    x2_apply(k)
                if p == 15:
                    xqT_copy(k)
                if p in (16, 17):
                    relu(k, p - 16)
                if p in (18, 19):
                    relu(k, p - 16)
                    h_round(k, p - 18)
                if p in (21, 22):
                    h_round(k, p - 19)
                if p == 24:
                    out_apply(k)

            def body(i, first, last):
                for p in range(2 * UNITS):
                    u, odd = divmod(p, 2)
                    n = UNITS * i + u
                    if not odd:
                        if u < UNITS - 2:
                            scores_copy(n + 2, (u + 2) % 4)
                        if not (first and u < 1):
                            exps(n - 1, (u - 1) % 4)
                    else:
                        if not (first and u < 2):
                            probsT_copy(n - 2, (u - 2) % 4)
                        if u % 4 == 2:
                            b = (u - 6) // 4
                            if b >= 0:
                                ctx_copy(i, b)
                            elif not first:
                                ctx_copy(i - 1, SB - 1)
                    if p == 6:
                        v_attn_copy(i)
                    if not last:
                        mixer_at(i + 1, p)
                    if not first:
                        ffn_at(i - 1, p)
                    if p >= 2 * UNITS - 2 and not last:
                        scores_copy(UNITS * (i + 1) + odd, odd)
                st.restart()

            for t, w in ((mixrep, head_mix.unsqueeze(1).broadcast_to([H, DH, H])),
                         (wout_sb, out_proj_w), (wq_sb, Wq), (wk_sb, Wk), (wv_sb, Wv), (wo_sb, Wo),
                         (bq_sb, col(bq)), (bk_sb, col(bk)), (bv_sb, col(bv)),
                         (bo_rep, bo.partition_broadcast(P))):
                a.dma_start(t[:, :], w).then_inc(q["wl_loaded"], 16)
            a.dma_start(w1_sb[:, :, :], w1.rearrange("(c p) d -> p c d", c=FC)).then_inc(q["f_loaded"], 16)
            a.dma_start(w2_sb[:, :], w2[:, :]).then_inc(q["f_loaded"], 16)
            a.dma_start(b1_sb[:, :], b1[:, :]).then_inc(q["f_loaded"], 16)
            a.dma_start(b2_sb[:, :], b2.rearrange("(o d) -> o d", o=1)).then_inc(q["f_loaded"], 16)
            squares(0)
            a.wait_ge(q["setup_pool"], 1)
            for p in range(1, 2 * UNITS):
                mixer_at(0, p)
            for u in range(2):
                scores_copy(u, u)
            a.wait_ge(q["ffn_wT"], 1)
            copy(w1T[:, :, :], ps_ffnA16[:, 0:HID].rearrange("p (c d) -> p c d", c=FC))
            copy(w2T[:, :, :], ps_ffnB16[:, 0:HID].rearrange("p (c d) -> p c d", c=FC)).then_inc(q["ffn_w"], 1)
            st.restart()
            body(0, True, False)
            with a.Fori(1, NBLK - 1) as i:
                body(i, False, False)
            body(NBLK - 1, False, True)
            n = UNITS * NBLK
            exps(n - 1, 3)
            probsT_copy(n - 2, 2)
            probsT_copy(n - 1, 3)
            ctx_copy(NBLK - 1, SB - 1)
            for p in range(2 * UNITS):
                ffn_at(NBLK - 1, p)

        @block.tensor
        def _(t):
            def tokens(b):
                return slice(S * b, S * (b + 1))

            def mm(out_, lhsT, rhs, start=True, stop=True):
                return t.matmul(out_, lhsT, rhs, start=start, stop=stop)

            def xs_turn(k):
                wait(t, q["q_ready"], k)
                t.wait_ge(q["xs_ready"], k + 1)
                for b in range(SB):
                    ins = t.transpose(ps_mixA[:, tokens(b)], xs[:, b, :], ident)
                ins.then_inc(q["xsT_ready"], 1)

            def conv(k):
                wait(t, q["k_ready"], k)
                t.wait_ge(q["xn_ready"], k + 1)
                for j in range(K):
                    ins = mm(seqs(ps_mixB), convdiag[:, j, :], xnp[:, :, j:j + S], start=(j == 0), stop=(j == K - 1))
                ins.then_inc(q["conv_ready"], 1)

            def project(k):
                t.wait_ge(q["xc_ready"], k + 1)
                mm(ps_mixA[:, :], win_sb[:, 0:D], xc[:, :]).then_inc(q["dtraw_ready"], 1)
                mm(ps_mixB[:, :], win_sb[:, D:2 * D], xc[:, :])
                mm(ps_mixC[:, :], wvswap.rearrange("p h d -> p (h d)"), xc[:, :]).then_inc(q["vraw_ready"], 1)

            def project_gate(k):
                t.wait_ge(q["v_copied"], k + 1)
                mm(ps_mixB[:, :], win_sb[:, 2 * D:3 * D], xc[:, :]).then_inc(q["graw_ready"], 1)

            def mix_heads(k):
                t.wait_ge(q["fin_ready"], k + 1)
                mm(ps_mixA[:, :], mixkron.rearrange("p h d -> p (h d)"), fin[:, :]).then_inc(q["mix_ready"], 1)

            def project_out(k):
                t.wait_ge(q["y_ready"], k + 1)
                for b in range(SB):
                    ins = mm(ps_mixC[:, tokens(b)], y[:, tokens(b)], wout_sb[:, :])
                ins.then_inc(q["outp_ready"], 1)

            def x1_turn(k):
                t.wait_ge(q["x1_ready"], k + 1)
                for b in range(SB):
                    ins = t.transpose(ps_mixA[:, tokens(b)], x1[:, b, :], ident)
                ins.then_inc(q["x1T_ready"], 1)

            def project_q(k):
                t.wait_ge(q["x1T_copied"], k + 1)
                mm(ps_mixA[:, :], wq_sb[:, :], x1T[:, :]).then_inc(q["qraw_ready"], 1)

            def ctx_turn(k):
                t.wait_ge(q["ctx_loaded"], 16 * (k + 1))
                t.wait_ge(q["stats1_ready"], k + 1)
                for b in range(SB):
                    ins = t.transpose(ps_mixC[:, tokens(b)], ctx_sb[:, b, :], ident)
                ins.then_inc(q["ctxT_ready"], 1)

            def project_k(k):
                t.wait_ge(q["ctxT_copied"], k + 1)
                mm(ps_mixB[:, :], wk_sb[:, :], ctxT[:, :]).then_inc(q["kraw_ready"], 1)

            def project_v(k):
                for b in range(SB):
                    ins = mm(ps_ffnA[:, tokens(b)], ctxT[:, tokens(b)], wv_sb[:, :])
                ins.then_inc(q["vps_ready"], 1)

            def scores(n, u):
                b, gr = divmod(u, NG)
                rows = slice(32 * gr, 32 * gr + 32)
                wait(t, q["scores_copied"], n)
                mm(ps_scores[:, :], qT[rows, tokens(b)], kmaskT[rows, b, :, :].rearrange("p j s -> p (j s)"))\
                    .then_inc(q["scores_ready"], 1)

            def probs_turn(n, r):
                wait(t, q["probsT_copied"], n)
                t.wait_ge(q["probs_ready"], n + 1)
                for j in range(HG):
                    ins = t.transpose(ps_probsT[:, tokens(j)], pr[:, r % 2, j, :], ident)
                ins.then_inc(q["probsT_ready"], 1)

            def times_v(n, u, k):
                b, gr = divmod(u, NG)
                if u == 0:
                    t.wait_ge(q["v_ready"], k + 1)
                if gr == 0:
                    wait(t, q["ctx_copied"], SB * k + b)
                t.wait_ge(q["probsT_copied"], n + 1)
                for j in range(HG):
                    h = HG * gr + j
                    ins = mm(ps_ctx[:, (DH + 1) * h:(DH + 1) * (h + 1)], prT[:, u % 2, j, :], vaug[:, b, h, :])
                ins.then_inc(q["pv_done"], 1)

            def on_turn(k):
                t.wait_ge(q["v_ready"], k + 2 if not isinstance(k, int) else min(k + 2, NBLK))
                t.wait_ge(q["on_ready"], SB * (k + 1))
                for b in range(SB):
                    ins = t.transpose(ps_ffnA[:, tokens(b)], on[:, b, :, :].rearrange("p h d -> p (h d)"), ident)
                ins.then_inc(q["onT_ready"], 1)

            def attn_out(k):
                t.wait_ge(q["oT_copied"], k + 1)
                for b in range(SB):
                    ins = mm(ps_ffnB[:, tokens(b)], oT[:, tokens(b)], wo_sb[:, :])
                ins.then_inc(q["attn_ready"], 1)

            def xq_turn(k):
                t.wait_ge(q["xq_ready"], k + 1)
                for b in range(SB):
                    ins = t.transpose(ps_ffnA16[:, tokens(b)], xq[:, b, :], ident16[:, :])
                ins.then_inc(q["xqT_ready"], 1)

            def hidden(k, c):
                if c == 0:
                    t.wait_ge(q["xqT_copied"], k + 1)
                if c >= 2:
                    t.wait_ge(q["relu_ready"], FC * k + c - 1)
                mm((ps_ffnB if c % 2 == 0 else ps_ffnA)[:, :], w1T[:, c, :], xqT[:, :]).then_inc(q["h_ready"], 1)

            def ffn_out(k):
                t.wait_ge(q["hq_ready"], FC * (k + 1))
                for b in range(SB):
                    for c in range(FC):
                        mm(ps_ffnA[:, tokens(b)], hq[:, c, tokens(b)], w2T[:, c, :], start=(c == 0), stop=False)
                    ins = mm(ps_ffnA[:, tokens(b)], ones_row[:, :], b2q[:, :], start=False, stop=True)
                ins.then_inc(q["out2_ready"], 1)

            def mixer_at(k, p):
                if p == 1:
                    xs_turn(k)
                if p == 2:
                    conv(k)
                if p == 6:
                    project(k)
                if p == 7:
                    project_gate(k)
                if p == 17:
                    mix_heads(k)
                if p == 18:
                    project_out(k)
                if p == 21:
                    x1_turn(k)
                if p == 22:
                    project_q(k)
                    ctx_turn(k)
                if p == 24:
                    project_k(k)

            def ffn_at(k, p):
                if p == 8:
                    on_turn(k)
                if p == 9:
                    attn_out(k)
                if p == 15:
                    xq_turn(k)
                if p in (16, 17, 18, 19):
                    hidden(k, p - 16)
                if p == 22:
                    ffn_out(k)

            def body(i, first, last):
                for p in range(2 * UNITS):
                    u, odd = divmod(p, 2)
                    n = UNITS * i + u
                    if not odd and u < UNITS - 2:
                        scores(n + 2, u + 2)
                    if odd:
                        if not (first and u < 2):
                            probs_turn(n - 2, (u - 2) % 4)
                        if u >= 3:
                            times_v(n - 3, u - 3, i)
                        elif not first:
                            times_v(n - 3, UNITS + u - 3, i - 1)
                    if p == 5:
                        project_v(i)
                    if not last:
                        mixer_at(i + 1, p)
                    if not first:
                        ffn_at(i - 1, p)
                    if p >= 2 * UNITS - 2 and not last:
                        if not odd:
                            t.wait_ge(q["q_ready"], i + 2)
                            t.wait_ge(q["k_ready"], i + 2)
                        scores(UNITS * (i + 1) + odd, odd)

            t.wait_ge(q["setup_pool"], 1)
            t.wait_ge(q["wl_loaded"], 16 * WL_LOADS)
            for p in range(1, 2 * UNITS):
                mixer_at(0, p)
            t.wait_ge(q["q_ready"], 1)
            t.wait_ge(q["k_ready"], 1)
            scores(0, 0)
            scores(1, 1)
            t.wait_ge(q["ffn_quant"], 1)
            for c in range(FC):
                t.transpose(ps_ffnA16[:, tokens(c)], w1q[:, c, :], ident16[:, :])
            for c in range(FC):
                ins = t.transpose(ps_ffnB16[:, tokens(c)], w2q[:, tokens(c)], ident16[:, :])
            ins.then_inc(q["ffn_wT"], 1)
            t.wait_ge(q["ffn_w"], 1)
            body(0, True, False)
            with t.Fori(1, NBLK - 1) as i:
                body(i, False, False)
            body(NBLK - 1, False, True)
            n = UNITS * NBLK
            probs_turn(n - 2, 2)
            times_v(n - 3, UNITS - 3, NBLK - 1)
            probs_turn(n - 1, 3)
            times_v(n - 2, UNITS - 2, NBLK - 1)
            times_v(n - 1, UNITS - 1, NBLK - 1)
            for p in range(2 * UNITS):
                ffn_at(NBLK - 1, p)


_INS = ['x', 'ctx_1024', 'L0_attn_norm_scale', 'L0_attn_conv_w', 'L0_attn_conv_b', 'L0_attn_in_proj_w',
        'L0_attn_dt_bias', 'L0_attn_head_mix', 'L0_attn_out_proj_w', 'L0_xattn_Wq', 'L0_xattn_bq',
        'L0_xattn_Wk', 'L0_xattn_bk', 'L0_xattn_Wv', 'L0_xattn_bv', 'L0_xattn_Wo', 'L0_xattn_bo',
        'L0_ffn_w1', 'L0_ffn_b1', 'L0_ffn_w2', 'L0_ffn_b2']


def kernel(**inputs):
    import numpy as _np
    import concourse.bacc as _bacc
    from concourse import mybir as _mybir
    from concourse.bass_utils import run_bass_kernel_spmd as _run

    nc = _bacc.Bacc("TRN2", target_bir_lowering=False, num_devices=1)
    arrays, args = {}, []
    for name in _INS:
        a = inputs[name]
        if name == 'L0_ffn_b1':
            a = _np.asarray(a).reshape(FC, P).T
        a = _np.ascontiguousarray(a)
        arrays[f"in_{name}"] = a
        args.append(nc.dram_tensor(f"in_{name}", a.shape, _mybir.dt.from_np(a.dtype), kind="ExternalInput").ap())
    c = constants()
    arrays["in_const"] = c
    args.append(nc.dram_tensor("in_const", c.shape, _mybir.dt.from_np(c.dtype), kind="ExternalInput").ap())
    args.append(nc.dram_tensor("out_0", (NSEQ, S, D), _mybir.dt.float32, kind="ExternalOutput").ap())
    decoder_kernel(nc, *args)
    r = _run(nc, [arrays], core_ids=[0])
    return r.results[0]["out_0"]
```

```python
from contextlib import ExitStack

import numpy as np

import concourse.bass as bass
from concourse import mybir

ALU = mybir.AluOpType
ACT = mybir.ActivationFunctionType
F32 = mybir.dt.float32
BF16 = mybir.dt.bfloat16

P = 128
NSEQ, S, D = 32, 128, 128
H = 16
DH = D // H
SB = 4
NBLK = NSEQ // SB
T = SB * S
HG = 4
NG = H // HG
UNITS = SB * NG
K = 4
CHUNK = 32
NCH = S // CHUNK
TOPK = max(16, S // 4)
ROUNDS = TOPK // 8
HID = 512
FC = HID // P
TAKEN = -3.0e38
SCALE = float(DH) ** -0.5
MAGIC = 1.5 * 2.0 ** 23
RMS_EPS, LN_EPS = 1e-6, 1e-5
EXP_FLOOR = -40.0
SP_CEIL = 30.0

C_ID, C_COS, C_SIN, C_HD, C_KM = 0, 128, 256, 384, 392
C_N = C_KM + NG


def constants():
    c = np.zeros((P, C_N), np.float32)
    c[:, C_ID:C_ID + P] = np.eye(P, dtype=np.float32)
    half = DH // 2
    inv = (1.0 / np.float32(10000.0) ** (np.arange(0, DH, 2, dtype=np.float32) / np.float32(DH))).astype(np.float32)
    freqs = np.arange(S, dtype=np.float32)[:, None] * inv[None, :]
    ch = np.arange(P)
    c[:, C_COS:C_COS + S] = np.cos(freqs).astype(np.float32).T[ch % half]
    sign = np.where(ch % DH < half, -1.0, 1.0).astype(np.float32)
    c[:, C_SIN:C_SIN + S] = np.sin(freqs).astype(np.float32).T[ch % half] * sign[:, None]
    c[ch, C_HD + ch % DH] = 1.0
    c[ch, C_KM + (ch // DH) % HG] = 1.0
    return c


class Steps:

    def __init__(self, eng, sem, held=None):
        self.eng, self.sem, self.held, self.n = eng, sem, held, 0

    def done(self, ins):
        ins.then_inc(self.sem, 1)
        self.n += 1
        return self.n

    def wait(self, n=None):
        self.eng.wait_ge(self.sem, self.n if n is None else n)

    def hold(self, sem, value):
        if isinstance(value, int) and value <= 0:
            return
        self.eng.wait_ge(sem, value)
        self.eng.nop().then_inc(self.held, 1)

    def restart(self):
        self.wait()
        self.eng.sem_clear(self.sem)
        self.n = 0


def wait(eng, sem, value):
    if isinstance(value, int) and value <= 0:
        return
    eng.wait_ge(sem, value)


V_NS, V_CW, V_CB, V_DT, V_BQ, V_BK, V_BV, V_B1, V_HM, V_BO = 0, 1, 5, 6, 7, 8, 9, 10, 14, 30
V_N = V_BO + D
W_OUT, W_Q, W_K, W_V, W_O = (D * j for j in range(5))


def decoder_kernel(nc, x, ctx, const, vectors, in_proj_w, weights, w1, w2, b2, out):
    with ExitStack() as es:
        def sb(name, shape, dt=F32):
            return es.enter_context(nc.sbuf_tensor(name, shape, dt))

        def bank(name):
            return es.enter_context(nc.psum_tensor(name, [P, T], F32))

        def sem(name):
            return es.enter_context(nc.semaphore(name))

        ps_scores, ps_probsT, ps_ctx = bank("ps_scores"), bank("ps_probsT"), bank("ps_ctx")
        ps_mixA, ps_mixB, ps_mixC = bank("ps_mixA"), bank("ps_mixB"), bank("ps_mixC")
        ps_ffnA, ps_ffnB = bank("ps_ffnA"), bank("ps_ffnB")
        ps_ffnA16 = ps_ffnA[:, :].bitcast(BF16)
        ps_ffnB16 = ps_ffnB[:, :].bitcast(BF16)

        cst = sb("cst", [P, C_N])
        ident = cst[:, C_ID:C_ID + P]
        ident16 = sb("ident16", [P, P], BF16)
        ident2, ident1024 = sb("ident2", [P, P]), sb("ident1024", [P, P])
        vec = sb("vec", [P, V_N])
        nscale, convb, dtb = (vec[:, c:c + 1] for c in (V_NS, V_CB, V_DT))
        bq_sb, bk_sb, bv_sb = (vec[:, c:c + 1] for c in (V_BQ, V_BK, V_BV))
        convw = vec[:, V_CW:V_CW + K]
        mixrep = vec[:, V_HM:V_HM + H]
        bo_rep = vec[:, V_BO:V_BO + D]
        win_sb = sb("win_sb", [P, 3 * D])
        wts = sb("wts", [P, 5 * D])
        wout_sb, wq_sb, wk_sb, wv_sb, wo_sb = (wts[:, c:c + D] for c in (W_OUT, W_Q, W_K, W_V, W_O))
        wvswap = sb("wvswap", [P, H, DH])
        convdiag = sb("convdiag", [P, K, P])
        mixkron = sb("mixkron", [P, H, DH])
        bkmask = sb("bkmask", [P, HG])
        w1_sb, w1_t, w1_u = sb("w1_sb", [P, FC, P]), sb("w1_t", [P, FC, P]), sb("w1_u", [P, FC, P])
        w2_sb, w2_t, w2_u = sb("w2_sb", [P, HID]), sb("w2_t", [P, HID]), sb("w2_u", [P, HID])
        w1q, w2q = sb("w1q", [P, FC, P], BF16), sb("w2q", [P, HID], BF16)
        w1T, w2T = sb("w1T", [P, FC, P], BF16), sb("w2T", [P, FC, P], BF16)
        b1_t, b1_u, b1_s = (sb(n, [P, FC]) for n in ("b1_t", "b1_u", "b1_s"))
        b2_sb, b2_t, b2_u = (sb(n, [1, D]) for n in ("b2_sb", "b2_t", "b2_u"))
        b2q = sb("b2q", [1, D], BF16)
        ones_row = sb("ones_row", [1, P], BF16)
        keep = sb("keep", [P, T])
        keepc = sb("keepc", [P, SB * NCH])
        neghalf = sb("neghalf", [P, SB])

        x_sb = sb("x_sb", [P, SB, D])
        sqjunk, ss = sb("sqjunk", [P, SB, D]), sb("ss", [P, SB])
        ms, rms = sb("ms", [P, SB]), sb("rms", [P, SB])
        xs, xnr = sb("xs", [P, SB, D]), sb("xnr", [P, T])
        xnp = sb("xnp", [P, SB, K - 1 + S])
        zc, ze, zl, zs, xc = (sb(n, [P, T]) for n in ("zc", "ze", "zl", "zs", "xc"))
        v_sb, vw_sb, ra, rb, vrot, vin = (sb(n, [P, T]) for n in ("v_sb", "vw_sb", "ra", "rb", "vrot", "vin"))
        dtc, dte, dts, dt_ = (sb(n, [P, T]) for n in ("dtc", "dte", "dts", "dt_"))
        gc, ge, gl, gate = (sb(n, [P, T]) for n in ("gc", "ge", "gl", "gate"))
        cum, cc, dst = (sb(n, [P, T]) for n in ("cum", "cc", "dst"))
        egrow, edecay, ecar = (sb(n, [P, T]) for n in ("egrow", "edecay", "ecar"))
        w_, cs, co, ce, fin = (sb(n, [P, T]) for n in ("w_", "cs", "co", "ce", "fin"))
        cdr, cd, cm, cn, eM, enM, seeds, cse, carr = (
            sb(n, [P, SB * NCH]) for n in ("cdr", "cd", "cm", "cn", "eM", "enM", "seeds", "cse", "carr"))
        mx, y = sb("mx", [P, T]), sb("y", [P, T])
        x1 = sb("x1", [P, SB, D])
        x1T = sb("x1T", [P, T])
        ctx_sb, ctxT = sb("ctx_sb", [P, SB, D]), sb("ctxT", [P, T])

        qT = sb("qT", [P, T])
        kmaskT = sb("kmaskT", [P, SB, HG, S])
        vaug = sb("vaug", [P, SB, H, DH + 1])
        sc_sb = sb("sc_sb", [P, 4, HG, S])
        rest = sb("rest", [P, 4, HG, S])
        top = sb("top", [P, 4, HG, TOPK])
        negmax = sb("negmax", [P, 4, HG])
        ex = sb("ex", [P, 2, HG, S])
        exr = sb("exr", [P, 2, HG, S])
        pr = sb("pr", [P, 2, HG, S])
        prT = sb("prT", [P, 2, HG, S])
        ctxo = sb("ctxo", [P, 2, H, DH + 1])
        rden = sb("rden", [P, 2, H])
        on = sb("on", [P, SB, H, DH])

        oT = sb("oT", [P, T])
        x1h, x2, out_sb = (sb(n, [P, SB, D]) for n in ("x1h", "x2", "out_sb"))
        q1, q2 = sb("q1", [P, SB, D]), sb("q2", [P, SB, D])
        xq, xqT = sb("xq", [P, SB, D], BF16), sb("xqT", [P, T], BF16)
        hr, hm, hu = sb("hr", [P, FC, T]), sb("hm", [P, FC, T]), sb("hu", [P, FC, T])
        magic, minus_magic = sb("magic", [P, 1]), sb("minus_magic", [P, 1])
        hq = sb("hq", [P, FC, T], BF16)
        bst = [sb(f"bst{n}", [P, SB, 6]) for n in range(3)]
        mv = [sb(f"mv{n}", [P, SB, 2]) for n in range(3)]
        ve = [sb(f"ve{n}", [P, SB]) for n in range(3)]
        rs = [sb(f"rs{n}", [P, SB]) for n in range(3)]
        nm = [sb(f"nm{n}", [P, SB]) for n in range(3)]
        nb = [sb(f"nb{n}", [P, SB]) for n in range(3)]

        names = """x_loaded ctx_loaded tables_loaded in_w_loaded w_loaded ffn_w_loaded out_free
            masks_set setup_done ffn_quant ffn_wT ffn_w
            ss_ready xs_ready xsT_ready xnr_ready xn_ready conv_ready zc_ready sig_ready xc_ready
            dtraw_ready vraw_ready v_copied dtc_ready graw_ready gc_ready softplus_ready dt_ready
            gate_ready cum_ready cc_ready dst_ready egrow_ready edecay_ready w_ready cdr_ready
            cn_ready em_ready cs_ready seeds_ready cse_ready fin_ready mix_ready mx_ready y_ready
            outp_ready stats1_ready ln1_ready x1_ready x1T_ready x1T_copied qraw_ready q_ready
            ctxT_ready ctxT_copied kraw_ready k_ready vps_ready v_ready
            scores_ready scores_copied topk_done negmax_ready exps_ready probs_ready
            probsT_ready probsT_copied pv_done ctx_copied rden_ready on_ready
            onT_ready oT_copied attn_ready x1h_ready stats2_ready ln2_ready x2_ready q1_ready xq_ready
            xqT_ready xqT_copied h_ready relu_ready hm_ready hq_ready out2_ready
            stats3_ready ln3_ready out_ready
            pool_steps dve_steps act_steps pool_held dve_held""".split()
        q = {n: sem(n) for n in names}

        x_v = x.rearrange("(k b) s d -> k s b d", b=SB)
        ctx_v = ctx.rearrange("(k b) s d -> k s b d", b=SB)
        out_v = out.rearrange("(k b) s d -> k s b d", b=SB)

        def col(v):
            return v.rearrange("(p o) -> p o", o=1)

        def seqs(t):
            return t.rearrange("p (b s) -> p b s", b=SB)

        def chunks(t):
            return t.rearrange("p (c s) -> p c s", s=CHUNK)

        block = es.enter_context(nc.Block())

        @block.sync
        def _(sp):
            def load_x(k):
                if not (isinstance(k, int) and k == 0):
                    sp.wait_ge(q["outp_ready"], k)
                sp.dma_start(x_sb[:, :, :], x_v[k]).then_inc(q["x_loaded"], 16)

            def load_ctx(k):
                if not (isinstance(k, int) and k == 0):
                    sp.wait_ge(q["ctxT_ready"], k)
                sp.dma_start(ctx_sb[:, :, :], ctx_v[k]).then_inc(q["ctx_loaded"], 16)

            def store(k):
                sp.wait_ge(q["out_ready"], k + 1)
                sp.dma_start(out_v[k], out_sb[:, :, :]).then_inc(q["out_free"], 16)

            load_x(0)
            sp.dma_start(win_sb[:, :], in_proj_w[:, :]).then_inc(q["in_w_loaded"], 16)
            sp.dma_start(wts[:, :], weights[:, :]).then_inc(q["w_loaded"], 16)
            load_ctx(0)
            sp.nop().then_inc(q["out_free"], 16)
            load_x(1)
            load_ctx(1)
            load_x(2)
            load_ctx(2)
            with sp.Fori(1, NBLK - 2) as i:
                load_x(i + 2)
                load_ctx(i + 2)
                store(i - 1)
            for k in range(NBLK - 3, NBLK):
                store(k)
            sp.wait_ge(q["out_free"], 16 * (NBLK + 1))

        @block.gpsimd
        def _(g):
            st = Steps(g, q["pool_steps"], q["pool_held"])

            def setup():
                st.done(g.memset(keep[:, :], 1.0))
                st.done(g.memset(keepc[:, :], 1.0))
                st.done(g.memset(neghalf[:, :], -0.5))
                st.done(g.memset(magic[:, :], MAGIC))
                st.done(g.memset(minus_magic[:, :], -MAGIC))
                st.done(g.memset(ones_row[:, :], 1.0))
                st.done(g.memset(xnp[:, :, 0:K - 1], 0.0))
                st.done(g.memset(carr[:, :], 0.0))
                st.done(g.memset(vaug[:, :, :, DH:DH + 1], 1.0))
                st.wait()
                st.done(g.memset(chunks(keep[:, :])[:, :, 0:1], 0.0))
                st.done(g.memset(keepc.rearrange("p (b c) -> p b c", b=SB)[:, :, 0:1], 0.0))
                st.wait()
                g.nop().then_inc(q["masks_set"], 1)

            def layernorm(n, stats, ready, k, eps=LN_EPS):
                st.hold(q[stats], k + 1)
                st.done(g.tensor_scalar(ve[n][:, :], mv[n][:, :, 1], eps, None, ALU.add))
                st.wait()
                st.done(g.tensor_tensor(rs[n][:, :], ve[n][:, :], neghalf[:, :], ALU.pow))
                st.wait()
                st.done(g.tensor_tensor(nm[n][:, :], mv[n][:, :, 0], rs[n][:, :], ALU.mult))
                st.wait()
                g.tensor_scalar(nb[n][:, :], nm[n][:, :], -1.0, None, ALU.mult).then_inc(q[ready], 1)

            def rms_scale(k):
                st.hold(q["ss_ready"], k + 1)
                st.done(g.tensor_scalar(ms[:, :], ss[:, :], 1.0 / D, RMS_EPS, ALU.mult, ALU.add))
                st.wait()
                st.done(g.tensor_tensor(rms[:, :], ms[:, :], neghalf[:, :], ALU.pow))
                st.wait()
                g.tensor_tensor(xs[:, :, :], x_sb[:, :, :], rms[:, :].unsqueeze(2).broadcast_to([P, SB, D]),
                                ALU.mult).then_inc(q["xs_ready"], 1)

            def clip_xn(k):
                st.hold(q["xnr_ready"], k + 1)
                g.tensor_scalar(xnp[:, :, K - 1:], seqs(xnr), 60000.0, -60000.0, ALU.min, ALU.max)\
                    .then_inc(q["xn_ready"], 1)

            def silu(k):
                g.wait_ge(q["sig_ready"], k + 1)
                g.tensor_tensor(xc[:, :], zc[:, :], zs[:, :], ALU.mult).then_inc(q["xc_ready"], 1)

            def rope(k):
                g.wait_ge(q["v_copied"], k + 1)
                st.done(g.tensor_tensor(seqs(ra), seqs(v_sb),
                                        cst[:, C_COS:C_COS + S].unsqueeze(1).broadcast_to([P, SB, S]), ALU.mult))
                st.done(g.tensor_tensor(seqs(rb), seqs(vw_sb),
                                        cst[:, C_SIN:C_SIN + S].unsqueeze(1).broadcast_to([P, SB, S]), ALU.mult))
                st.wait()
                st.done(g.tensor_tensor(vrot[:, :], ra[:, :], rb[:, :], ALU.add))

            def clip_dt(k):
                st.hold(q["softplus_ready"], k + 1)
                g.tensor_scalar(dt_[:, :], dts[:, :], 2.0, 0.001, ALU.min, ALU.max).then_inc(q["dt_ready"], 1)
                st.wait()
                g.wait_ge(q["dt_ready"], k + 1)
                st.done(g.tensor_tensor(vin[:, :], vrot[:, :], dt_[:, :], ALU.mult))

            def decay(k):
                st.hold(q["cum_ready"], k + 1)
                g.tensor_scalar(cc[:, :], cum[:, :], 20.0, None, ALU.min).then_inc(q["cc_ready"], 1)
                g.wait_ge(q["cc_ready"], k + 1)
                g.tensor_tensor(chunks(dst), chunks(cc),
                                chunks(cc)[:, :, 0:1].broadcast_to([P, SB * NCH, CHUNK]), ALU.subtract)\
                    .then_inc(q["dst_ready"], 1)

            def grow(k):
                st.wait()
                g.wait_ge(q["egrow_ready"], k + 1)
                g.tensor_tensor(w_[:, :], egrow[:, :], vin[:, :], ALU.mult).then_inc(q["w_ready"], 1)

            def chunk_decay(k):
                st.hold(q["cdr_ready"], k + 1)
                st.done(g.tensor_scalar(cd[:, :], cdr[:, :], 80.0, None, ALU.min))
                st.wait()
                cdv = cd.rearrange("p (b c) -> p b c", b=SB)
                st.done(g.tensor_tensor(cm.rearrange("p (b c) -> p b c", b=SB), cdv,
                                        cdv[:, :, 0:1].broadcast_to([P, SB, NCH]), ALU.subtract))
                st.wait()
                g.tensor_scalar(cn[:, :], cm[:, :], 20.0, None, ALU.min).then_inc(q["cn_ready"], 1)

            def chunk_out(k):
                g.wait_ge(q["edecay_ready"], k + 1)
                g.wait_ge(q["cs_ready"], k + 1)
                n = st.done(g.tensor_tensor(co[:, :], edecay[:, :], cs[:, :], ALU.mult))
                g.wait_ge(q["em_ready"], k + 1)
                st.wait(n)
                g.tensor_tensor(seeds[:, :], chunks(co)[:, :, CHUNK - 1], eM[:, :], ALU.mult)\
                    .then_inc(q["seeds_ready"], 1)

            def carry(k):
                g.wait_ge(q["cse_ready"], k + 1)
                cv, sv, ev = (t.rearrange("p (b c) -> p b c", b=SB) for t in (carr, cse, enM))
                st.done(g.tensor_tensor(cv[:, :, 1:NCH], sv[:, :, 0:NCH - 1], ev[:, :, 1:NCH], ALU.mult))
                st.wait()
                st.done(g.tensor_tensor(chunks(ce), chunks(ecar),
                                        carr[:, :].unsqueeze(2).broadcast_to([P, SB * NCH, CHUNK]), ALU.mult))
                st.wait()
                g.tensor_tensor(fin[:, :], co[:, :], ce[:, :], ALU.add).then_inc(q["fin_ready"], 1)

            def gated(k):
                g.wait_ge(q["gate_ready"], k + 1)
                g.wait_ge(q["mx_ready"], k + 1)
                g.tensor_tensor(y[:, :], mx[:, :], gate[:, :], ALU.mult).then_inc(q["y_ready"], 1)

            def neg_max(n, r):
                st.hold(q["topk_done"], n + 1)
                g.tensor_scalar(negmax[:, r, :], top[:, r, :, 0], -SCALE, None, ALU.mult)\
                    .then_inc(q["negmax_ready"], 1)

            def probs(n, r):
                wait(g, q["probsT_ready"], n - 1)
                g.wait_ge(q["exps_ready"], n + 1)
                g.tensor_tensor(pr[:, r % 2, :, :], ex[:, r % 2, :, :], exr[:, r % 2, :, :], ALU.subtract)\
                    .then_inc(q["probs_ready"], 1)

            def normalise(k, b):
                g.wait_ge(q["rden_ready"], SB * k + b + 1)
                if b == 0:
                    wait(g, q["onT_ready"], k)
                g.tensor_tensor(on[:, b, :, :], ctxo[:, b % 2, :, 0:DH],
                                rden[:, b % 2, :].unsqueeze(2).broadcast_to([P, H, DH]), ALU.mult)\
                    .then_inc(q["on_ready"], 1)

            def residual(k):
                g.wait_ge(q["x1_ready"], k + 1)
                wait(g, q["attn_ready"], k)
                g.tensor_tensor(x1h[:, :, :], x1[:, :, :], bo_rep.unsqueeze(1).broadcast_to([P, SB, D]),
                                ALU.add).then_inc(q["x1h_ready"], 1)

            def clip_x2(k):
                st.hold(q["x2_ready"], k + 1)
                g.tensor_scalar(q1[:, :, :], x2[:, :, :], 127.0 / 16, -8.0, ALU.min, ALU.max)\
                    .then_inc(q["q1_ready"], 1)

            def clip_hidden(k, c):
                st.hold(q["relu_ready"], FC * k + c + 1)
                g.tensor_scalar(hm[:, c, :], hr[:, c, :], 127.0, None, ALU.min).then_inc(q["hm_ready"], 1)

            def body(i, first, last):
                mixer, ffn = not last, not first
                for p in range(2 * UNITS):
                    u, odd = divmod(p, 2)
                    n, r = UNITS * i + u - 1, (u - 1) % 4
                    unit = not (first and u < 1)
                    if unit and not odd:
                        neg_max(n, r)
                    if odd and u % 4 == 3:
                        b = (u - 7) // 4
                        if b >= 0:
                            normalise(i, b)
                        elif not first:
                            normalise(i - 1, SB - 1)
                    if mixer:
                        mixer_at(i + 1, p)
                    if ffn:
                        ffn_at(i - 1, p)
                    if p == 16:
                        residual(i)
                    if unit and odd:
                        probs(n, r)
                st.restart()

            def mixer_at(k, p):
                if p == 0:
                    rms_scale(k)
                if p == 2:
                    clip_xn(k)
                if p == 7:
                    silu(k)
                if p == 10:
                    rope(k)
                if p == 11:
                    clip_dt(k)
                if p == 13:
                    decay(k)
                if p == 14:
                    grow(k)
                if p == 13:
                    chunk_decay(k)
                if p == 18:
                    chunk_out(k)
                if p == 20:
                    carry(k)
                if p == 22:
                    gated(k)
                if p == 24:
                    layernorm(0, "stats1_ready", "ln1_ready", k)

            def ffn_at(k, p):
                if p == 12:
                    layernorm(1, "stats2_ready", "ln2_ready", k)
                if p == 14:
                    clip_x2(k)
                if p in (18, 19, 20, 21):
                    clip_hidden(k, p - 18)
                if p == 26:
                    layernorm(2, "stats3_ready", "ln3_ready", k, eps=LN_EPS * 2.0 ** 20)

            setup()
            for p in range(2 * UNITS):
                mixer_at(0, p)
            st.restart()
            body(0, True, False)
            with g.Fori(1, NBLK - 1) as i:
                body(i, False, False)
            body(NBLK - 1, False, True)
            n = UNITS * NBLK - 1
            neg_max(n, 3)
            probs(n, 3)
            normalise(NBLK - 1, SB - 1)
            for p in range(2 * UNITS):
                ffn_at(NBLK - 1, p)

        @block.vector
        def _(v):
            st = Steps(v, q["dve_steps"], q["dve_held"])

            def top_rounds(n, r, rounds):
                if 0 in rounds:
                    wait_n = n + 1
                    st.hold(q["scores_copied"], wait_n)
                    st.hold(q["exps_ready"], n - 3)
                for rd in rounds:
                    base = st.n
                    for j in range(HG):
                        src = sc_sb[:, r, j, :] if rd == 0 else rest[:, r, j, :]
                        if rd > 0:
                            st.wait(mr[j])
                        mx8[j] = st.done(v.max(top[:, r, j, 8 * rd:8 * rd + 8], src))
                    for j in range(HG):
                        src = sc_sb[:, r, j, :] if rd == 0 else rest[:, r, j, :]
                        st.wait(mx8[j])
                        ins = v.match_replace(rest[:, r, j, :], top[:, r, j, 8 * rd:8 * rd + 8], src, TAKEN)
                        if rd == ROUNDS - 1 and j == HG - 1:
                            ins.then_inc(q["topk_done"], 1)
                        else:
                            mr[j] = st.done(ins)

            mr, mx8 = [0] * HG, [0] * HG

            def moments(n, made, src, ready, k):
                v.wait_ge(q[made], k + 1)
                for b in range(SB):
                    first = st.done(v.bn_stats(bst[n][:, b, :], src[:, S * b:S * (b + 1)]))
                for b in range(SB):
                    st.wait(first - SB + 1 + b)
                    ins = v.bn_aggr(mv[n][:, b, :], bst[n][:, b, :])
                    if b < SB - 1:
                        st.done(ins)
                ins.then_inc(q[ready], 1)

            def conv_clamp(k):
                v.wait_ge(q["conv_ready"], k + 1)
                v.tensor_scalar(zc[:, :], ps_mixB[:, :], convb, EXP_FLOOR, ALU.add, ALU.max)\
                    .then_inc(q["zc_ready"], 1)

            def dt_clamp(k):
                v.wait_ge(q["dtraw_ready"], k + 1)
                v.tensor_scalar(dtc[:, :], ps_mixA[:, :], dtb, SP_CEIL, ALU.add, ALU.min)\
                    .then_inc(q["dtc_ready"], 1)

            def gate_clamp(k):
                v.wait_ge(q["graw_ready"], k + 1)
                v.tensor_scalar(gc[:, :], ps_mixB[:, :], EXP_FLOOR, None, ALU.max).then_inc(q["gc_ready"], 1)

            def scan(ready, out_, keep_, in_, sem_, k):
                v.wait_ge(q[ready], k + 1)
                v.tensor_tensor_scan(out_, keep_, in_, 0.0, ALU.mult, ALU.add).then_inc(q[sem_], 1)

            def recip(k, b):
                v.wait_ge(q["ctx_copied"], SB * k + b + 1)
                v.reciprocal(rden[:, b % 2, :], ctxo[:, b % 2, :, DH]).then_inc(q["rden_ready"], 1)

            def mixer_at(k, p):
                if p == 6:
                    conv_clamp(k)
                if p == 10:
                    dt_clamp(k)
                if p == 11:
                    gate_clamp(k)
                if p == 13:
                    scan("dt_ready", cum[:, :], keep[:, :], dt_[:, :], "cum_ready", k)
                if p == 15:
                    scan("cc_ready", cdr[:, :], keepc[:, :], chunks(cc)[:, :, CHUNK - 1], "cdr_ready", k)
                if p == 17:
                    scan("w_ready", cs[:, :], keep[:, :], w_[:, :], "cs_ready", k)
                if p == 20:
                    scan("seeds_ready", cse[:, :], keepc[:, :], seeds[:, :], "cse_ready", k)
                if p == 24:
                    moments(0, "outp_ready", ps_mixC, "stats1_ready", k)

            def ffn_at(k, p):
                if p == 12:
                    moments(1, "attn_ready", ps_ffnB, "stats2_ready", k)
                if p == 26:
                    moments(2, "out2_ready", ps_ffnA, "stats3_ready", k)

            def body(i, first, last):
                for p in range(2 * UNITS):
                    u, odd = divmod(p, 2)
                    if odd and u % 4 == 3:
                        b = (u - 7) // 4
                        if b >= 0:
                            recip(i, b)
                        elif not first:
                            recip(i - 1, SB - 1)
                    if not last:
                        mixer_at(i + 1, p)
                    if not first:
                        ffn_at(i - 1, p)
                    half = ROUNDS // 2
                    top_rounds(UNITS * i + u, u % 4, range(half, ROUNDS) if odd else range(half))
                st.restart()

            def quantise_weight(src, t, u, out_, factor=1.0):
                st.done(v.tensor_scalar(t, src, 64.0, 127.0, ALU.mult, ALU.min))
                st.wait()
                st.done(v.tensor_scalar(u, t, -128.0, MAGIC, ALU.max, ALU.add))
                st.wait()
                st.done(v.tensor_scalar(out_, u, -MAGIC, factor, ALU.add, ALU.mult))

            v.wait_ge(q["tables_loaded"], 32)
            for j in range(K):
                st.done(v.tensor_scalar(convdiag[:, j, :], ident, convw[:, j:j + 1], None, ALU.mult))
            st.done(v.tensor_scalar(ident2[:, :], ident, 2.0, None, ALU.mult))
            st.done(v.tensor_scalar(ident1024[:, :], ident, 1024.0, None, ALU.mult))
            st.done(v.tensor_copy(ident16[:, :], ident))
            st.done(v.tensor_tensor(mixkron[:, :, :], mixrep.unsqueeze(2).broadcast_to([P, H, DH]),
                                    cst[:, C_HD:C_HD + DH].unsqueeze(1).broadcast_to([P, H, DH]), ALU.mult))
            st.done(v.tensor_scalar(bkmask[:, :], cst[:, C_KM:C_KM + HG], bk_sb, None, ALU.mult))
            v.wait_ge(q["in_w_loaded"], 16)
            wv = win_sb[:, D:2 * D].rearrange("p (h d) -> p h d", h=H)
            st.done(v.tensor_copy(wvswap[:, :, 0:DH // 2], wv[:, :, DH // 2:DH]))
            st.done(v.tensor_copy(wvswap[:, :, DH // 2:DH], wv[:, :, 0:DH // 2]))
            st.wait()
            v.nop().then_inc(q["setup_done"], 1)
            v.wait_ge(q["ffn_w_loaded"], 48)
            quantise_weight(w1_sb[:, :, :], w1_t[:, :, :], w1_u[:, :, :], w1q[:, :, :])
            quantise_weight(w2_sb[:, :], w2_t[:, :], w2_u[:, :], w2q[:, :])
            quantise_weight(vec[:, V_B1:V_B1 + FC], b1_t[:, :], b1_u[:, :], b1_s[:, :], 0.25)
            quantise_weight(b2_sb[:, :], b2_t[:, :], b2_u[:, :], b2q[:, :], 16.0)
            st.wait()
            v.nop().then_inc(q["ffn_quant"], 1)
            for p in range(2 * UNITS):
                if p == 3:
                    v.wait_ge(q["masks_set"], 1)
                mixer_at(0, p)
            st.restart()
            body(0, True, False)
            with v.Fori(1, NBLK - 1) as i:
                body(i, False, False)
            body(NBLK - 1, False, True)
            recip(NBLK - 1, SB - 1)
            for p in range(2 * UNITS):
                ffn_at(NBLK - 1, p)

        @block.scalar
        def _(a):
            st = Steps(a, q["act_steps"])

            def copy(out_, in_, bias=0.0, scale=1.0):
                return a.activation(out_, in_, ACT.Identity, bias=bias, scale=scale)

            def sigmoid(src, e, l, out_, ready):
                st.done(a.activation(e, src, ACT.Exp, scale=-1.0))
                st.wait()
                st.done(a.activation(l, e, ACT.Ln, bias=1.0))
                st.wait()
                a.activation(out_, l, ACT.Exp, scale=-1.0).then_inc(q[ready], 1)

            def apply_norm(n, src, out_, ready):
                for b in range(SB):
                    ins = copy(out_[:, b, :], src[:, S * b:S * (b + 1)], bias=nb[n][:, b:b + 1], scale=rs[n][:, b:b + 1])
                ins.then_inc(q[ready], 1)

            def squares(k):
                a.wait_ge(q["x_loaded"], 16 * (k + 1))
                for b in range(SB):
                    ins = a.activation(sqjunk[:, b, :], x_sb[:, b, :], ACT.Square, accum_out=ss[:, b:b + 1])
                ins.then_inc(q["ss_ready"], 1)

            def xn_copy(k):
                a.wait_ge(q["xsT_ready"], k + 1)
                copy(xnr[:, :], ps_mixA[:, :], scale=nscale).then_inc(q["xnr_ready"], 1)

            def conv_sigmoid(k):
                a.wait_ge(q["zc_ready"], k + 1)
                sigmoid(zc[:, :], ze[:, :], zl[:, :], zs[:, :], "sig_ready")

            def v_copy(k):
                a.wait_ge(q["vraw_ready"], k + 1)
                copy(v_sb[:, :], ps_mixB[:, :])
                copy(vw_sb[:, :], ps_mixC[:, :]).then_inc(q["v_copied"], 1)

            def softplus(k):
                a.wait_ge(q["dtc_ready"], k + 1)
                st.done(a.activation(dte[:, :], dtc[:, :], ACT.Exp))
                st.wait()
                a.activation(dts[:, :], dte[:, :], ACT.Ln, bias=1.0).then_inc(q["softplus_ready"], 1)

            def gate_sigmoid(k):
                a.wait_ge(q["gc_ready"], k + 1)
                sigmoid(gc[:, :], ge[:, :], gl[:, :], gate[:, :], "gate_ready")

            def decays(k):
                a.wait_ge(q["dst_ready"], k + 1)
                a.activation(egrow[:, :], dst[:, :], ACT.Exp).then_inc(q["egrow_ready"], 1)
                a.activation(edecay[:, :], dst[:, :], ACT.Exp, scale=-1.0).then_inc(q["edecay_ready"], 1)
                st.done(a.activation(ecar[:, :], cc[:, :], ACT.Exp, scale=-1.0))

            def chunk_exps(k):
                a.wait_ge(q["cn_ready"], k + 1)
                st.done(a.activation(eM[:, :], cn[:, :], ACT.Exp))
                st.done(a.activation(enM[:, :], cn[:, :], ACT.Exp, scale=-1.0))
                st.wait()
                a.nop().then_inc(q["em_ready"], 1)

            def mx_copy(k):
                a.wait_ge(q["mix_ready"], k + 1)
                copy(mx[:, :], ps_mixA[:, :]).then_inc(q["mx_ready"], 1)

            def x1_apply(k):
                wait(a, q["x1h_ready"], k)
                a.wait_ge(q["ln1_ready"], k + 1)
                apply_norm(0, ps_mixC, x1, "x1_ready")

            def x1T_copy(k):
                a.wait_ge(q["x1T_ready"], k + 1)
                copy(x1T[:, :], ps_mixA[:, :]).then_inc(q["x1T_copied"], 1)

            def ctxT_copy(k):
                wait(a, q["vps_ready"], k)
                a.wait_ge(q["ctxT_ready"], k + 1)
                copy(ctxT[:, :], ps_mixC[:, :]).then_inc(q["ctxT_copied"], 1)

            def q_copy(k):
                wait(a, q["scores_ready"], UNITS * k)
                a.wait_ge(q["qraw_ready"], k + 1)
                copy(qT[:, :], ps_mixA[:, :], bias=bq_sb).then_inc(q["q_ready"], 1)

            def k_copy(k):
                a.wait_ge(q["kraw_ready"], k + 1)
                for j in range(HG):
                    ins = copy(kmaskT[:, :, j, :], seqs(ps_mixB), bias=bkmask[:, j:j + 1],
                               scale=cst[:, C_KM + j:C_KM + j + 1])
                ins.then_inc(q["k_ready"], 1)

            def v_attn_copy(k):
                wait(a, q["pv_done"], UNITS * k)
                a.wait_ge(q["vps_ready"], k + 1)
                copy(vaug[:, :, :, 0:DH], ps_ffnA.rearrange("p (b h d) -> p b h d", b=SB, h=H))\
                    .then_inc(q["v_ready"], 1)

            def scores_copy(n, r):
                wait(a, q["exps_ready"], n - 3)
                a.wait_ge(q["scores_ready"], n + 1)
                copy(sc_sb[:, r, :, :], ps_scores.rearrange("p (j s) -> p j s", j=HG))\
                    .then_inc(q["scores_copied"], 1)

            def exps(n, r):
                wait(a, q["probs_ready"], n - 1)
                a.wait_ge(q["negmax_ready"], n + 1)
                for j in range(HG):
                    ins = a.activation(ex[:, r % 2, j, :], sc_sb[:, r, j, :], ACT.Exp,
                                       bias=negmax[:, r, j:j + 1], scale=SCALE)
                for j in range(HG):
                    ins = a.activation(exr[:, r % 2, j, :], rest[:, r, j, :], ACT.Exp,
                                       bias=negmax[:, r, j:j + 1], scale=SCALE)
                ins.then_inc(q["exps_ready"], 1)

            def probsT_copy(n, r):
                wait(a, q["pv_done"], n - 1)
                a.wait_ge(q["probsT_ready"], n + 1)
                copy(prT[:, r % 2, :, :], ps_probsT.rearrange("p (j s) -> p j s", j=HG))\
                    .then_inc(q["probsT_copied"], 1)

            def ctx_copy(k, b):
                wait(a, q["on_ready"], SB * k + b - 1)
                a.wait_ge(q["pv_done"], UNITS * k + NG * (b + 1))
                copy(ctxo[:, b % 2, :, :], ps_ctx[:, 0:H * (DH + 1)].rearrange("p (h d) -> p h d", h=H))\
                    .then_inc(q["ctx_copied"], 1)

            def oT_copy(k):
                a.wait_ge(q["onT_ready"], k + 1)
                copy(oT[:, :], ps_ffnA[:, :], bias=bv_sb).then_inc(q["oT_copied"], 1)

            def x2_apply(k):
                a.wait_ge(q["ln2_ready"], k + 1)
                apply_norm(1, ps_ffnB, x2, "x2_ready")

            def x2_round(k):
                a.wait_ge(q["q1_ready"], k + 1)
                st.done(copy(q2[:, :, :], q1[:, :, :], bias=magic[:, :], scale=16.0))
                st.wait()
                copy(xq[:, :, :], q2[:, :, :], bias=minus_magic[:, :]).then_inc(q["xq_ready"], 1)

            def xqT_copy(k):
                a.wait_ge(q["xqT_ready"], k + 1)
                copy(xqT[:, :], ps_ffnA16[:, 0:T]).then_inc(q["xqT_copied"], 1)

            def relu(k, c):
                a.wait_ge(q["h_ready"], FC * k + c + 1)
                a.activation(hr[:, c, :], (ps_ffnB if c % 2 == 0 else ps_ffnA)[:, :], ACT.Relu,
                             bias=b1_s[:, c:c + 1], scale=1.0 / 64).then_inc(q["relu_ready"], 1)

            def h_round(k, c):
                a.wait_ge(q["hm_ready"], FC * k + c + 1)
                st.done(copy(hu[:, c, :], hm[:, c, :], bias=magic[:, :]))
                st.wait()
                copy(hq[:, c, :], hu[:, c, :], bias=minus_magic[:, :]).then_inc(q["hq_ready"], 1)

            def out_apply(k):
                a.wait_ge(q["out_free"], 16 * (k + 1))
                a.wait_ge(q["ln3_ready"], k + 1)
                apply_norm(2, ps_ffnA, out_sb, "out_ready")

            def mixer_at(k, p):
                if p == 0:
                    squares(k)
                if p == 2:
                    xn_copy(k)
                if p == 6:
                    conv_sigmoid(k)
                if p == 9:
                    v_copy(k)
                if p == 10:
                    softplus(k)
                if p == 12:
                    gate_sigmoid(k)
                if p == 14:
                    decays(k)
                if p == 16:
                    chunk_exps(k)
                if p == 22:
                    mx_copy(k)
                if p == 25:
                    x1_apply(k)
                if p == 26:
                    x1T_copy(k)
                if p == 27:
                    ctxT_copy(k)
                if p == 28:
                    q_copy(k)
                    k_copy(k)

            def ffn_at(k, p):
                if p == 8:
                    oT_copy(k)
                if p == 13:
                    x2_apply(k)
                if p == 14:
                    x2_round(k)
                if p == 16:
                    xqT_copy(k)
                if p in (17, 18, 19, 20):
                    relu(k, p - 17)
                if p in (20, 21, 22, 23):
                    h_round(k, p - 20)
                if p == 27:
                    out_apply(k)

            def body(i, first, last):
                for p in range(2 * UNITS):
                    u, odd = divmod(p, 2)
                    n = UNITS * i + u
                    if not odd and u < UNITS - 2:
                        scores_copy(n + 2, (u + 2) % 4)
                    if p == 6:
                        v_attn_copy(i)
                    if not last:
                        mixer_at(i + 1, p)
                    if not first:
                        ffn_at(i - 1, p)
                    if not odd:
                        if not (first and u < 1):
                            exps(n - 1, (u - 1) % 4)
                    else:
                        if not (first and u < 2):
                            probsT_copy(n - 2, (u - 2) % 4)
                        if u % 4 == 2:
                            b = (u - 6) // 4
                            if b >= 0:
                                ctx_copy(i, b)
                            elif not first:
                                ctx_copy(i - 1, SB - 1)
                    if p >= 2 * UNITS - 2 and not last:
                        scores_copy(UNITS * (i + 1) + odd, odd)
                st.restart()

            a.dma_start(cst[:, :], const[:, :]).then_inc(q["tables_loaded"], 16)
            a.dma_start(vec[:, :], vectors[:, :]).then_inc(q["tables_loaded"], 16)
            a.dma_start(w1_sb[:, :, :], w1.rearrange("(c p) d -> p c d", c=FC)).then_inc(q["ffn_w_loaded"], 16)
            a.dma_start(w2_sb[:, :], w2[:, :]).then_inc(q["ffn_w_loaded"], 16)
            a.dma_start(b2_sb[:, :], b2.rearrange("(o d) -> o d", o=1)).then_inc(q["ffn_w_loaded"], 16)
            a.preload_act_table_set("natural_log_exp_and_others")
            squares(0)
            a.wait_ge(q["tables_loaded"], 32)
            for p in range(1, 2 * UNITS):
                mixer_at(0, p)
            for u in range(2):
                scores_copy(u, u)
            a.wait_ge(q["ffn_wT"], 1)
            copy(w1T[:, :, :], ps_ffnA16[:, 0:HID].rearrange("p (c d) -> p c d", c=FC))
            copy(w2T[:, :, :], ps_ffnB16[:, 0:HID].rearrange("p (c d) -> p c d", c=FC)).then_inc(q["ffn_w"], 1)
            st.restart()
            body(0, True, False)
            with a.Fori(1, NBLK - 1) as i:
                body(i, False, False)
            body(NBLK - 1, False, True)
            n = UNITS * NBLK
            exps(n - 1, 3)
            probsT_copy(n - 2, 2)
            probsT_copy(n - 1, 3)
            ctx_copy(NBLK - 1, SB - 1)
            for p in range(2 * UNITS):
                ffn_at(NBLK - 1, p)

        @block.tensor
        def _(t):
            def tokens(b):
                return slice(S * b, S * (b + 1))

            def mm(out_, lhsT, rhs, start=True, stop=True):
                return t.matmul(out_, lhsT, rhs, start=start, stop=stop)

            def xs_turn(k):
                wait(t, q["q_ready"], k)
                t.wait_ge(q["xs_ready"], k + 1)
                for b in range(SB):
                    ins = t.transpose(ps_mixA[:, tokens(b)], xs[:, b, :], ident)
                ins.then_inc(q["xsT_ready"], 1)

            def conv(k):
                wait(t, q["k_ready"], k)
                t.wait_ge(q["xn_ready"], k + 1)
                for j in range(K):
                    ins = mm(seqs(ps_mixB), convdiag[:, j, :], xnp[:, :, j:j + S], start=(j == 0), stop=(j == K - 1))
                ins.then_inc(q["conv_ready"], 1)

            def project(k):
                t.wait_ge(q["xc_ready"], k + 1)
                mm(ps_mixA[:, :], win_sb[:, 0:D], xc[:, :]).then_inc(q["dtraw_ready"], 1)
                mm(ps_mixB[:, :], win_sb[:, D:2 * D], xc[:, :])
                mm(ps_mixC[:, :], wvswap.rearrange("p h d -> p (h d)"), xc[:, :]).then_inc(q["vraw_ready"], 1)

            def project_gate(k):
                t.wait_ge(q["v_copied"], k + 1)
                mm(ps_mixB[:, :], win_sb[:, 2 * D:3 * D], xc[:, :]).then_inc(q["graw_ready"], 1)

            def mix_heads(k):
                t.wait_ge(q["fin_ready"], k + 1)
                mm(ps_mixA[:, :], mixkron.rearrange("p h d -> p (h d)"), fin[:, :]).then_inc(q["mix_ready"], 1)

            def project_out(k):
                t.wait_ge(q["y_ready"], k + 1)
                for b in range(SB):
                    mm(ps_mixC[:, tokens(b)], ident2[:, :], x_sb[:, b, :], stop=False)
                    ins = mm(ps_mixC[:, tokens(b)], y[:, tokens(b)], wout_sb, start=False)
                ins.then_inc(q["outp_ready"], 1)

            def x1_turn(k):
                t.wait_ge(q["x1_ready"], k + 1)
                for b in range(SB):
                    ins = t.transpose(ps_mixA[:, tokens(b)], x1[:, b, :], ident)
                ins.then_inc(q["x1T_ready"], 1)

            def project_q(k):
                t.wait_ge(q["x1T_copied"], k + 1)
                mm(ps_mixA[:, :], wq_sb, x1T[:, :]).then_inc(q["qraw_ready"], 1)

            def ctx_turn(k):
                t.wait_ge(q["ctx_loaded"], 16 * (k + 1))
                t.wait_ge(q["x1_ready"], k + 1)
                for b in range(SB):
                    ins = t.transpose(ps_mixC[:, tokens(b)], ctx_sb[:, b, :], ident)
                ins.then_inc(q["ctxT_ready"], 1)

            def project_k(k):
                t.wait_ge(q["ctxT_copied"], k + 1)
                mm(ps_mixB[:, :], wk_sb, ctxT[:, :]).then_inc(q["kraw_ready"], 1)

            def project_v(k):
                for b in range(SB):
                    ins = mm(ps_ffnA[:, tokens(b)], ctxT[:, tokens(b)], wv_sb)
                ins.then_inc(q["vps_ready"], 1)

            def scores(n, u):
                b, gr = divmod(u, NG)
                rows = slice(32 * gr, 32 * gr + 32)
                wait(t, q["scores_copied"], n)
                mm(ps_scores[:, :], qT[rows, tokens(b)], kmaskT[rows, b, :, :].rearrange("p j s -> p (j s)"))\
                    .then_inc(q["scores_ready"], 1)

            def probs_turn(n, r):
                wait(t, q["probsT_copied"], n)
                t.wait_ge(q["probs_ready"], n + 1)
                for j in range(HG):
                    ins = t.transpose(ps_probsT[:, tokens(j)], pr[:, r % 2, j, :], ident)
                ins.then_inc(q["probsT_ready"], 1)

            def times_v(n, u, k):
                b, gr = divmod(u, NG)
                if u == 0:
                    t.wait_ge(q["v_ready"], k + 1)
                if gr == 0:
                    wait(t, q["ctx_copied"], SB * k + b)
                t.wait_ge(q["probsT_copied"], n + 1)
                for j in range(HG):
                    h = HG * gr + j
                    ins = mm(ps_ctx[:, (DH + 1) * h:(DH + 1) * (h + 1)], prT[:, u % 2, j, :], vaug[:, b, h, :])
                ins.then_inc(q["pv_done"], 1)

            def on_turn(k):
                t.wait_ge(q["v_ready"], k + 2 if not isinstance(k, int) else min(k + 2, NBLK))
                t.wait_ge(q["on_ready"], SB * (k + 1))
                for b in range(SB):
                    ins = t.transpose(ps_ffnA[:, tokens(b)], on[:, b, :, :].rearrange("p h d -> p (h d)"), ident)
                ins.then_inc(q["onT_ready"], 1)

            def attn_out(k):
                t.wait_ge(q["x1h_ready"], k + 1)
                t.wait_ge(q["oT_copied"], k + 1)
                for b in range(SB):
                    mm(ps_ffnB[:, tokens(b)], ident, x1h[:, b, :], stop=False)
                    ins = mm(ps_ffnB[:, tokens(b)], oT[:, tokens(b)], wo_sb, start=False)
                ins.then_inc(q["attn_ready"], 1)

            def xq_turn(k):
                t.wait_ge(q["xq_ready"], k + 1)
                for b in range(SB):
                    ins = t.transpose(ps_ffnA16[:, tokens(b)], xq[:, b, :], ident16[:, :])
                ins.then_inc(q["xqT_ready"], 1)

            def hidden(k, c):
                if c == 0:
                    t.wait_ge(q["xqT_copied"], k + 1)
                if c >= 2:
                    t.wait_ge(q["relu_ready"], FC * k + c - 1)
                mm((ps_ffnB if c % 2 == 0 else ps_ffnA)[:, :], w1T[:, c, :], xqT[:, :]).then_inc(q["h_ready"], 1)

            def ffn_out(k):
                t.wait_ge(q["hq_ready"], FC * (k + 1))
                for b in range(SB):
                    mm(ps_ffnA[:, tokens(b)], ident1024[:, :], x2[:, b, :], stop=False)
                    for c in range(FC):
                        mm(ps_ffnA[:, tokens(b)], hq[:, c, tokens(b)], w2T[:, c, :], start=False, stop=False)
                    ins = mm(ps_ffnA[:, tokens(b)], ones_row[:, :], b2q[:, :], start=False, stop=True)
                ins.then_inc(q["out2_ready"], 1)

            def mixer_at(k, p):
                if p == 1:
                    xs_turn(k)
                if p == 3:
                    conv(k)
                if p == 8:
                    project(k)
                if p == 9:
                    project_gate(k)
                if p == 21:
                    mix_heads(k)
                if p == 22:
                    project_out(k)
                if p == 26:
                    x1_turn(k)
                if p == 26:
                    ctx_turn(k)
                    project_q(k)
                if p == 27:
                    project_k(k)

            def ffn_at(k, p):
                if p == 8:
                    on_turn(k)
                if p == 9:
                    attn_out(k)
                if p == 16:
                    xq_turn(k)
                if p in (17, 18, 19, 20):
                    hidden(k, p - 17)
                if p == 24:
                    ffn_out(k)

            def body(i, first, last):
                for p in range(2 * UNITS):
                    u, odd = divmod(p, 2)
                    n = UNITS * i + u
                    if not odd and u < UNITS - 2:
                        scores(n + 2, u + 2)
                    if odd:
                        if not (first and u < 2):
                            probs_turn(n - 2, (u - 2) % 4)
                        if u >= 3:
                            times_v(n - 3, u - 3, i)
                        elif not first:
                            times_v(n - 3, UNITS + u - 3, i - 1)
                    if p == 5:
                        project_v(i)
                    if not last:
                        mixer_at(i + 1, p)
                    if not first:
                        ffn_at(i - 1, p)
                    if p >= 2 * UNITS - 2 and not last:
                        if not odd:
                            t.wait_ge(q["q_ready"], i + 2)
                            t.wait_ge(q["k_ready"], i + 2)
                        scores(UNITS * (i + 1) + odd, odd)

            t.wait_ge(q["tables_loaded"], 32)
            for p in range(1, 2 * UNITS):
                if p == 2:
                    t.wait_ge(q["setup_done"], 1)
                    t.wait_ge(q["w_loaded"], 16)
                mixer_at(0, p)
            t.wait_ge(q["q_ready"], 1)
            t.wait_ge(q["k_ready"], 1)
            scores(0, 0)
            scores(1, 1)
            t.wait_ge(q["ffn_quant"], 1)
            for c in range(FC):
                t.transpose(ps_ffnA16[:, tokens(c)], w1q[:, c, :], ident16[:, :])
            for c in range(FC):
                ins = t.transpose(ps_ffnB16[:, tokens(c)], w2q[:, tokens(c)], ident16[:, :])
            ins.then_inc(q["ffn_wT"], 1)
            t.wait_ge(q["ffn_w"], 1)
            body(0, True, False)
            with t.Fori(1, NBLK - 1) as i:
                body(i, False, False)
            body(NBLK - 1, False, True)
            n = UNITS * NBLK
            probs_turn(n - 2, 2)
            times_v(n - 3, UNITS - 3, NBLK - 1)
            probs_turn(n - 1, 3)
            times_v(n - 2, UNITS - 2, NBLK - 1)
            times_v(n - 1, UNITS - 1, NBLK - 1)
            for p in range(2 * UNITS):
                ffn_at(NBLK - 1, p)


def kernel(**inputs):
    import numpy as _np
    import concourse.bacc as _bacc
    from concourse import mybir as _mybir
    from concourse.bass_utils import run_bass_kernel_spmd as _run

    def arr(name):
        return _np.asarray(inputs[name])

    vectors = _np.concatenate([
        arr('L0_attn_norm_scale')[:, None], arr('L0_attn_conv_w')[:, 0, :], arr('L0_attn_conv_b')[:, None],
        arr('L0_attn_dt_bias')[:, None], arr('L0_xattn_bq')[:, None], arr('L0_xattn_bk')[:, None],
        arr('L0_xattn_bv')[:, None], arr('L0_ffn_b1').reshape(FC, P).T,
        _np.repeat(arr('L0_attn_head_mix'), DH, axis=0),
        _np.broadcast_to(arr('L0_xattn_bo')[None, :], (P, D))], axis=1)
    weights = _np.concatenate([arr('L0_attn_out_proj_w'), arr('L0_xattn_Wq'), arr('L0_xattn_Wk'),
                               arr('L0_xattn_Wv'), arr('L0_xattn_Wo')], axis=1)
    laid_out = {'x': arr('x'), 'ctx': arr('ctx_1024'), 'const': constants(), 'vectors': vectors,
                'in_proj_w': arr('L0_attn_in_proj_w'), 'weights': weights, 'w1': arr('L0_ffn_w1'),
                'w2': arr('L0_ffn_w2'), 'b2': arr('L0_ffn_b2')}
    nc = _bacc.Bacc("TRN2", target_bir_lowering=False, num_devices=1)
    arrays, args = {}, []
    for name, a in laid_out.items():
        a = _np.ascontiguousarray(a)
        arrays[f"in_{name}"] = a
        args.append(nc.dram_tensor(f"in_{name}", a.shape, _mybir.dt.from_np(a.dtype), kind="ExternalInput").ap())
    args.append(nc.dram_tensor("out_0", (NSEQ, S, D), _mybir.dt.float32, kind="ExternalOutput").ap())
    decoder_kernel(nc, *args)
    r = _run(nc, [arrays], core_ids=[0])
    return r.results[0]["out_0"]
```

```python
from contextlib import ExitStack

import numpy as np

import concourse.bass as bass
from concourse import mybir

ALU = mybir.AluOpType
ACT = mybir.ActivationFunctionType
F32 = mybir.dt.float32
BF16 = mybir.dt.bfloat16

P = 128
NSEQ, S, D = 32, 128, 128
H = 16
DH = D // H
SB = 4
NBLK = NSEQ // SB
T = SB * S
HG = 4
NG = H // HG
UNITS = SB * NG
K = 4
CHUNK = 32
NCH = S // CHUNK
TOPK = max(16, S // 4)
ROUNDS = TOPK // 8
HID = 512
FC = HID // P
TAKEN = -3.0e38
SCALE = float(DH) ** -0.5
MAGIC = 1.5 * 2.0 ** 23
RMS_EPS, LN_EPS = 1e-6, 1e-5
EPS = (LN_EPS, LN_EPS, LN_EPS * 2.0 ** 20)
EXP_CEIL = 2.0 ** 60

C_ID, C_COS, C_SIN, C_HD, C_KM = 0, 128, 256, 384, 392
C_N = C_KM + NG


def constants():
    c = np.zeros((P, C_N), np.float32)
    c[:, C_ID:C_ID + P] = np.eye(P, dtype=np.float32)
    half = DH // 2
    inv = (1.0 / np.float32(10000.0) ** (np.arange(0, DH, 2, dtype=np.float32) / np.float32(DH))).astype(np.float32)
    freqs = np.arange(S, dtype=np.float32)[:, None] * inv[None, :]
    ch = np.arange(P)
    c[:, C_COS:C_COS + S] = np.cos(freqs).astype(np.float32).T[ch % half]
    sign = np.where(ch % DH < half, -1.0, 1.0).astype(np.float32)
    c[:, C_SIN:C_SIN + S] = np.sin(freqs).astype(np.float32).T[ch % half] * sign[:, None]
    c[ch, C_HD + ch % DH] = 1.0
    c[ch, C_KM + (ch // DH) % HG] = 1.0
    return c


class Steps:

    def __init__(self, eng, sem, held=None):
        self.eng, self.sem, self.held, self.n = eng, sem, held, 0

    def done(self, ins):
        ins.then_inc(self.sem, 1)
        self.n += 1
        return self.n

    def wait(self, n=None):
        self.eng.wait_ge(self.sem, self.n if n is None else n)

    def hold(self, sem, value):
        if isinstance(value, int) and value <= 0:
            return
        self.eng.wait_ge(sem, value)
        self.eng.nop().then_inc(self.held, 1)

    def restart(self):
        self.wait()
        self.eng.sem_clear(self.sem)
        self.n = 0


def wait(eng, sem, value):
    if isinstance(value, int) and value <= 0:
        return
    eng.wait_ge(sem, value)


V_NS, V_CW, V_CB, V_DT, V_BQ, V_BK, V_BV, V_B1, V_HM, V_BO = 0, 1, 5, 6, 7, 8, 9, 10, 14, 30
V_N = V_BO + D
W_OUT, W_Q, W_K, W_V, W_O = (D * j for j in range(5))


def decoder_kernel(nc, x, ctx, const, vectors, in_proj_w, weights, w1, w2, b2, out):
    with ExitStack() as es:
        def sb(name, shape, dt=F32):
            return es.enter_context(nc.sbuf_tensor(name, shape, dt))

        def bank(name):
            return es.enter_context(nc.psum_tensor(name, [P, T], F32))

        def sem(name):
            return es.enter_context(nc.semaphore(name))

        ps_scores, ps_probsT, ps_ctx = bank("ps_scores"), bank("ps_probsT"), bank("ps_ctx")
        ps_mixA, ps_mixB, ps_mixC = bank("ps_mixA"), bank("ps_mixB"), bank("ps_mixC")
        ps_ffnA, ps_ffnB = bank("ps_ffnA"), bank("ps_ffnB")
        ps_ffnA16 = ps_ffnA[:, :].bitcast(BF16)
        ps_ffnB16 = ps_ffnB[:, :].bitcast(BF16)
        EARLY, LATE = range(SB - 1), range(SB - 1, SB)
        HEADS_BANK = {"": ps_ffnA, "early_": ps_mixA}
        ATTN_BANK = {"": ps_ffnB, "early_": ps_mixB}
        XQ_BANK = {"": ps_ffnA16, "early_": ps_mixC[:, :].bitcast(BF16)}
        EARLY_HIDDEN = (ps_scores, ps_mixA, ps_mixB, ps_scores)
        LATE_HIDDEN = (ps_ffnB, ps_ffnA, ps_probsT, ps_ctx)
        EARLY_OUT, LATE_OUT = ps_mixC, ps_mixA

        cst = sb("cst", [P, C_N])
        ident = cst[:, C_ID:C_ID + P]
        ident16 = sb("ident16", [P, P], BF16)
        ident2, ident1024 = sb("ident2", [P, P]), sb("ident1024", [P, P])
        vec = sb("vec", [P, V_N])
        nscale, convb, dtb = (vec[:, c:c + 1] for c in (V_NS, V_CB, V_DT))
        bq_sb, bk_sb, bv_sb = (vec[:, c:c + 1] for c in (V_BQ, V_BK, V_BV))
        convw = vec[:, V_CW:V_CW + K]
        mixrep = vec[:, V_HM:V_HM + H]
        bo_rep = vec[:, V_BO:V_BO + D]
        win_sb = sb("win_sb", [P, 3 * D])
        wts = sb("wts", [P, 5 * D])
        wout_sb, wq_sb, wk_sb, wv_sb, wo_sb = (wts[:, c:c + D] for c in (W_OUT, W_Q, W_K, W_V, W_O))
        wvswap = sb("wvswap", [P, H, DH])
        convdiag = sb("convdiag", [P, K, P])
        mixkron = sb("mixkron", [P, H, DH])
        bkmask = sb("bkmask", [P, HG])
        w1_sb, w1_t, w1_u = sb("w1_sb", [P, FC, P]), sb("w1_t", [P, FC, P]), sb("w1_u", [P, FC, P])
        w2_sb = sb("w2_sb", [P, HID])
        w2_t, w2_u = (w.rearrange("p c q -> p (c q)") for w in (w1_t, w1_u))
        w1q, w2q = sb("w1q", [P, FC, P], BF16), sb("w2q", [P, HID], BF16)
        w1T, w2T = sb("w1T", [P, FC, P], BF16), sb("w2T", [P, FC, P], BF16)
        b1_t, b1_u, b1_s = (sb(n, [P, FC]) for n in ("b1_t", "b1_u", "b1_s"))
        b2_sb, b2_t, b2_u = (sb(n, [1, D]) for n in ("b2_sb", "b2_t", "b2_u"))
        b2q = sb("b2q", [1, D], BF16)
        ones_row = sb("ones_row", [1, P], BF16)
        keep = sb("keep", [P, T])
        keepc = sb("keepc", [P, SB * NCH])
        neghalf = sb("neghalf", [P, SB])
        eps_sb, ln_var = sb("eps_sb", [P, 4]), sb("ln_var", [P, SB])

        x_sb = sb("x_sb", [P, SB, D])
        junk, ss = sb("junk", [P, SB, D]), sb("ss", [P, SB])
        ms, rms = sb("ms", [P, SB]), sb("rms", [P, SB])
        xs, xnr = sb("xs", [P, SB, D]), sb("xnr", [P, T])
        xnp = sb("xnp", [P, SB, K - 1 + S])
        z, ze, zm, zl, zs, xc = (sb(n, [P, T]) for n in ("z", "ze", "zm", "zl", "zs", "xc"))
        ncb = sb("ncb", [P, 1])
        v_sb, vw_sb, ra, rb, vrot, vin = (sb(n, [P, T]) for n in ("v_sb", "vw_sb", "ra", "rb", "vrot", "vin"))
        dte, dtm, dts, dt_ = (sb(n, [P, T]) for n in ("dte", "dtm", "dts", "dt_"))
        ge, gm, gl, gate = (sb(n, [P, T]) for n in ("ge", "gm", "gl", "gate"))
        cum, cc, dst = (sb(n, [P, T]) for n in ("cum", "cc", "dst"))
        egrow, edecay, ecar = (sb(n, [P, T]) for n in ("egrow", "edecay", "ecar"))
        w_, cs, co, ce, fin = (sb(n, [P, T]) for n in ("w_", "cs", "co", "ce", "fin"))
        cdr, cd, cm, cn, eM, enM, seeds, cse, carr = (
            sb(n, [P, SB * NCH]) for n in ("cdr", "cd", "cm", "cn", "eM", "enM", "seeds", "cse", "carr"))
        mx, y = sb("mx", [P, T]), sb("y", [P, T])
        x1 = sb("x1", [P, SB, D])
        x1T = sb("x1T", [P, T])
        ctx_sb, ctxT = sb("ctx_sb", [P, SB, D]), sb("ctxT", [P, T])

        qT = sb("qT", [P, T])
        kmaskT = sb("kmaskT", [P, SB, HG, S])
        vaug = sb("vaug", [P, SB, H, DH + 1])
        sc_sb = sb("sc_sb", [P, 4, HG, S])
        rest = sb("rest", [P, 4, HG, S])
        top = sb("top", [P, 4, HG, TOPK])
        negmax = sb("negmax", [P, 4, HG])
        ex = sb("ex", [P, 2, HG, S])
        exr = sb("exr", [P, 2, HG, S])
        pr = sb("pr", [P, 2, HG, S])
        prT = sb("prT", [P, 2, HG, S])
        ctxo = sb("ctxo", [P, 2, H, DH + 1])
        rden = sb("rden", [P, 2, H])
        on = sb("on", [P, SB, H, DH])

        oT = sb("oT", [P, T])
        x1h, x2, out_sb = (sb(n, [P, SB, D]) for n in ("x1h", "x2", "out_sb"))
        q1, q2 = sb("q1", [P, SB, D]), sb("q2", [P, SB, D])
        xq, xqT = sb("xq", [P, SB, D], BF16), sb("xqT", [P, T], BF16)
        hr, hu = sb("hr", [P, FC, T]), sb("hu", [P, FC, T])
        magic, minus_magic = sb("magic", [P, 1]), sb("minus_magic", [P, 1])
        hq = sb("hq", [P, FC, T], BF16)
        bst = [sb(f"bst{n}", [P, SB, 6]) for n in range(3)]
        mv = [sb(f"mv{n}", [P, SB, 2]) for n in range(3)]
        ve = [sb(f"ve{n}", [P, SB]) for n in range(3)]
        rs = [sb(f"rs{n}", [P, SB]) for n in range(3)]
        total, nmean, spread = ([sb(f"{a}{n}", [P, SB]) for n in range(3)] for a in ("total", "nmean", "spread"))
        nb = [sb(f"nb{n}", [P, SB]) for n in range(3)]

        names = """x_loaded ctx_loaded tables_loaded in_w_loaded w_loaded ffn_w_loaded out_free
            masks_set setup_done ffn_quant ffn_wT ffn_w
            ss_ready rms_ready rstd_ready xs_ready xsT_ready xnr_ready xn_ready conv_ready ze_ready zm_ready
            sig_ready xc_ready dtraw_ready vraw_ready v_copied dte_ready dtm_ready graw_ready ge_ready gm_ready
            softplus_ready dt_ready
            gate_ready cum_ready cc_ready dst_ready egrow_ready edecay_ready w_ready cdr_ready
            cn_ready em_ready cs_ready seeds_ready cse_ready fin_ready mix_ready mx_ready y_ready
            first_mix_ready first_mx_ready first_y_ready first_outp_ready first_stats0_ready first_rstd_ready
            first_ln0_ready first_x1_ready first_x1T_ready first_x1T_copied first_qraw_ready first_q_ready
            outp_ready sum0_ready nmean0_ready stats0_ready ln0_ready
            x1_ready x1T_ready x1T_copied qraw_ready q_ready
            ctxT_ready ctxT_copied kraw_ready k_ready vps_ready v_ready
            scores_ready scores_copied topk_done negmax_ready exps_ready probs_ready
            probsT_ready probsT_copied pv_done ctx_copied rden_ready on_ready
            onT_ready oT_copied attn_ready x1h_ready sum1_ready nmean1_ready stats1_ready ln1_ready
            x2_ready q1_ready xq_ready xqT_ready xqT_copied h_ready relu_ready hu_ready hq_ready out2_ready
            sum2_ready nmean2_ready stats2_ready ln2_ready out_ready
            early_onT_ready early_oT_copied early_attn_ready early_stats1_ready early_rstd_ready early_ln1_ready
            early_x2_ready early_xq_ready early_xqT_ready early_xqT_copied early_h_ready early_relu_ready early_hq_ready
            early_out2_ready early_stats2_ready early_ln2_ready early_out_ready
            pool_steps dve_steps act_steps pool_held dve_held""".split()
        q = {n: sem(n) for n in names}

        x_v = x.rearrange("(k b) s d -> k s b d", b=SB)
        ctx_v = ctx.rearrange("(k b) s d -> k s b d", b=SB)
        out_v = out.rearrange("(k b) s d -> k s b d", b=SB)

        def seqs(t):
            return t.rearrange("p (b s) -> p b s", b=SB)

        def chunks(t):
            return t.rearrange("p (c s) -> p c s", s=CHUNK)

        ALL = range(SB)
        FIRST, OTHERS = range(1), range(1, SB)

        def made(k, early):
            return 1 if early else k + 1

        MIX_BANK = {"": ps_mixA, "first_": ps_probsT}
        OUT_BANK = {"": ps_mixC, "first_": ps_ctx}
        TURN_BANK = {"": ps_mixA, "first_": ps_ffnA}

        def span(which):
            return slice(S * which[0], S * (which[-1] + 1))

        block = es.enter_context(nc.Block())

        @block.sync
        def _(sp):
            def load_x(k):
                if not (isinstance(k, int) and k == 0):
                    sp.wait_ge(q["outp_ready"], k)
                sp.dma_start(x_sb[:, :, :], x_v[k]).then_inc(q["x_loaded"], 16)

            def load_ctx(k):
                if not (isinstance(k, int) and k == 0):
                    sp.wait_ge(q["ctxT_ready"], k)
                sp.dma_start(ctx_sb[:, :, :], ctx_v[k]).then_inc(q["ctx_loaded"], 16)

            def store(k):
                sp.wait_ge(q["out_ready"], k + 1)
                sp.dma_start(out_v[k], out_sb[:, :, :]).then_inc(q["out_free"], 16)

            load_x(0)
            sp.dma_start(win_sb[:, :], in_proj_w[:, :]).then_inc(q["in_w_loaded"], 16)
            sp.dma_start(wts[:, :], weights[:, :]).then_inc(q["w_loaded"], 16)
            load_ctx(0)
            sp.nop().then_inc(q["out_free"], 16)
            load_x(1)
            load_ctx(1)
            load_x(2)
            load_ctx(2)
            with sp.Fori(1, NBLK - 2) as i:
                load_x(i + 2)
                load_ctx(i + 2)
                store(i - 1)
            for k in range(NBLK - 3, NBLK - 1):
                store(k)
            for part, ready, count in ((EARLY, "early_out_ready", 1), (LATE, "out_ready", NBLK)):
                b0, b1 = part[0], part[-1] + 1
                sp.wait_ge(q[ready], count)
                sp.dma_start(out_v[NBLK - 1, :, b0:b1], out_sb[:, b0:b1, :]).then_inc(q["out_free"], 16)
            sp.wait_ge(q["out_free"], 16 * (NBLK + 2))

        class Products:

            def __init__(self, e, st):
                self.e, self.st = e, st

            def negative_mean(self, n, k):
                self.st.hold(q[f"sum{n}_ready"], k + 1 - (n == 0))
                self.e.tensor_scalar(nmean[n][:, :], total[n][:, :], -1.0 / D, None, ALU.mult)\
                    .then_inc(q[f"nmean{n}_ready"], 1)

            def layernorm(self, n, k):
                self.st.hold(q[f"stats{n}_ready"], k + 1)
                self.st.done(self.e.tensor_scalar(ve[n][:, :], spread[n][:, :], 1.0 / D, EPS[n], ALU.mult, ALU.add))
                self.st.wait()
                self.st.done(self.e.tensor_tensor(rs[n][:, :], ve[n][:, :], neghalf[:, :], ALU.pow))
                self.st.wait()
                self.e.tensor_tensor(nb[n][:, :], nmean[n][:, :], rs[n][:, :], ALU.mult)\
                    .then_inc(q[f"ln{n}_ready"], 1)

            def rms_factor(self, k):
                self.st.hold(q["ss_ready"], k + 1)
                self.st.done(self.e.tensor_scalar(ms[:, :], ss[:, :], 1.0 / D, RMS_EPS, ALU.mult, ALU.add))
                self.st.wait()
                self.e.tensor_tensor(rms[:, :], ms[:, :], neghalf[:, :], ALU.pow).then_inc(q["rms_ready"], 1)

            def rms_scale(self, k):
                self.e.wait_ge(q["rms_ready"], k + 1)
                self.e.tensor_tensor(xs[:, :, :], x_sb[:, :, :], rms[:, :].unsqueeze(2).broadcast_to([P, SB, D]),
                                     ALU.mult).then_inc(q["xs_ready"], 1)

            def clip_xn(self, k):
                self.st.hold(q["xnr_ready"], k + 1)
                self.e.tensor_scalar(xnp[:, :, K - 1:], seqs(xnr), 60000.0, -60000.0, ALU.min, ALU.max)\
                    .then_inc(q["xn_ready"], 1)

            def cap(self, out_, in_, made, ready, k):
                self.st.hold(q[made], k + 1)
                self.e.tensor_scalar(out_[:, :], in_[:, :], EXP_CEIL, None, ALU.min).then_inc(q[ready], 1)

            def silu(self, k):
                self.e.wait_ge(q["sig_ready"], k + 1)
                self.e.tensor_tensor(xc[:, :], z[:, :], zs[:, :], ALU.mult).then_inc(q["xc_ready"], 1)

            def rope(self, k):
                self.e.wait_ge(q["v_copied"], k + 1)
                self.st.done(self.e.tensor_tensor(
                    seqs(ra), seqs(v_sb), cst[:, C_COS:C_COS + S].unsqueeze(1).broadcast_to([P, SB, S]), ALU.mult))
                self.st.done(self.e.tensor_tensor(
                    seqs(rb), seqs(vw_sb), cst[:, C_SIN:C_SIN + S].unsqueeze(1).broadcast_to([P, SB, S]), ALU.mult))
                self.st.wait()
                self.st.done(self.e.tensor_tensor(vrot[:, :], ra[:, :], rb[:, :], ALU.add))

            def clip_dt(self, k):
                self.st.hold(q["softplus_ready"], k + 1)
                self.e.tensor_scalar(dt_[:, :], dts[:, :], 2.0, 0.001, ALU.min, ALU.max).then_inc(q["dt_ready"], 1)

            def step_input(self, k):
                self.st.wait()
                self.e.wait_ge(q["dt_ready"], k + 1)
                self.st.done(self.e.tensor_tensor(vin[:, :], vrot[:, :], dt_[:, :], ALU.mult))

            def decay(self, k):
                self.st.hold(q["cum_ready"], k + 1)
                self.e.tensor_scalar(cc[:, :], cum[:, :], 20.0, None, ALU.min).then_inc(q["cc_ready"], 1)
                self.e.wait_ge(q["cc_ready"], k + 1)
                self.e.tensor_tensor(chunks(dst), chunks(cc),
                                     chunks(cc)[:, :, 0:1].broadcast_to([P, SB * NCH, CHUNK]), ALU.subtract)\
                    .then_inc(q["dst_ready"], 1)

            def grow(self, k):
                self.st.wait()
                self.e.wait_ge(q["egrow_ready"], k + 1)
                self.e.tensor_tensor(w_[:, :], egrow[:, :], vin[:, :], ALU.mult).then_inc(q["w_ready"], 1)

            def chunk_decay(self, k):
                self.st.hold(q["cdr_ready"], k + 1)
                self.st.done(self.e.tensor_scalar(cd[:, :], cdr[:, :], 80.0, None, ALU.min))
                self.st.wait()
                cdv = cd.rearrange("p (b c) -> p b c", b=SB)
                self.st.done(self.e.tensor_tensor(cm.rearrange("p (b c) -> p b c", b=SB), cdv,
                                                  cdv[:, :, 0:1].broadcast_to([P, SB, NCH]), ALU.subtract))
                self.st.wait()
                self.e.tensor_scalar(cn[:, :], cm[:, :], 20.0, None, ALU.min).then_inc(q["cn_ready"], 1)

            def chunk_out(self, k):
                self.e.wait_ge(q["edecay_ready"], k + 1)
                self.e.wait_ge(q["cs_ready"], k + 1)
                n = self.st.done(self.e.tensor_tensor(co[:, :], edecay[:, :], cs[:, :], ALU.mult))
                self.e.wait_ge(q["em_ready"], k + 1)
                self.st.wait(n)
                self.e.tensor_tensor(seeds[:, :], chunks(co)[:, :, CHUNK - 1], eM[:, :], ALU.mult)\
                    .then_inc(q["seeds_ready"], 1)

            def carry(self, k):
                self.e.wait_ge(q["cse_ready"], k + 1)
                cv, sv, ev = (t.rearrange("p (b c) -> p b c", b=SB) for t in (carr, cse, enM))
                self.st.done(self.e.tensor_tensor(cv[:, :, 1:NCH], sv[:, :, 0:NCH - 1], ev[:, :, 1:NCH], ALU.mult))
                self.st.wait()
                self.st.done(self.e.tensor_tensor(chunks(ce), chunks(ecar),
                                                  carr[:, :].unsqueeze(2).broadcast_to([P, SB * NCH, CHUNK]), ALU.mult))
                self.st.wait()
                self.e.tensor_tensor(fin[:, :], co[:, :], ce[:, :], ALU.add).then_inc(q["fin_ready"], 1)

            def gated(self, k, which=ALL, first=""):
                self.e.wait_ge(q["gate_ready"], k + 1)
                self.e.wait_ge(q[first + "mx_ready"], k + 1)
                self.e.tensor_tensor(y[:, span(which)], mx[:, span(which)], gate[:, span(which)], ALU.mult)\
                    .then_inc(q[first + "y_ready"], 1)

            def neg_max(self, n, r):
                self.st.hold(q["topk_done"], n + 1)
                self.e.tensor_scalar(negmax[:, r, :], top[:, r, :, 0], -SCALE, None, ALU.mult)\
                    .then_inc(q["negmax_ready"], 1)

            def probs(self, n, r):
                wait(self.e, q["probsT_ready"], n - 1)
                self.e.wait_ge(q["exps_ready"], n + 1)
                self.e.tensor_tensor(pr[:, r % 2, :, :], ex[:, r % 2, :, :], exr[:, r % 2, :, :], ALU.subtract)\
                    .then_inc(q["probs_ready"], 1)

            def normalise(self, k, b):
                self.e.wait_ge(q["rden_ready"], SB * k + b + 1)
                if b == 0:
                    wait(self.e, q["onT_ready"], k)
                self.e.tensor_tensor(on[:, b, :, :], ctxo[:, b % 2, :, 0:DH],
                                     rden[:, b % 2, :].unsqueeze(2).broadcast_to([P, H, DH]), ALU.mult)\
                    .then_inc(q["on_ready"], 1)

        @block.gpsimd
        def _(g):
            st = Steps(g, q["pool_steps"], q["pool_held"])
            do = Products(g, st)

            def setup():
                st.done(g.memset(keep[:, :], 1.0))
                st.done(g.memset(keepc[:, :], 1.0))
                st.done(g.memset(neghalf[:, :], -0.5))
                for n in range(3):
                    st.done(g.memset(eps_sb[:, n:n + 1], EPS[n]))
                st.done(g.memset(eps_sb[:, 3:4], RMS_EPS))
                st.done(g.memset(magic[:, :], MAGIC))
                st.done(g.memset(minus_magic[:, :], -MAGIC))
                st.done(g.memset(ones_row[:, :], 1.0))
                st.done(g.memset(xnp[:, :, 0:K - 1], 0.0))
                st.done(g.memset(carr[:, :], 0.0))
                st.done(g.memset(vaug[:, :, :, DH:DH + 1], 1.0))
                st.wait()
                st.done(g.memset(chunks(keep[:, :])[:, :, 0:1], 0.0))
                st.done(g.memset(keepc.rearrange("p (b c) -> p b c", b=SB)[:, :, 0:1], 0.0))
                st.wait()
                g.nop().then_inc(q["masks_set"], 1)

            def residual(k):
                g.wait_ge(q["x1_ready"], k + 1)
                wait(g, q["attn_ready"], k)
                g.tensor_tensor(x1h[:, :, :], x1[:, :, :], bo_rep.unsqueeze(1).broadcast_to([P, SB, D]),
                                ALU.add).then_inc(q["x1h_ready"], 1)

            def clip_x2(k):
                st.hold(q["x2_ready"], k + 1)
                g.tensor_scalar(q1[:, :, :], x2[:, :, :], 127.0 / 16, -8.0, ALU.min, ALU.max)\
                    .then_inc(q["q1_ready"], 1)

            def clip_hidden(k, c):
                st.hold(q["relu_ready"], FC * k + c + 1)
                g.tensor_scalar(hu[:, c, :], hr[:, c, :], 127.0, MAGIC, ALU.min, ALU.add)\
                    .then_inc(q["hu_ready"], 1)

            def body(i, first, last):
                mixer, ffn = not last, not first
                for p in range(2 * UNITS):
                    u, odd = divmod(p, 2)
                    n, r = UNITS * i + u - 1, (u - 1) % 4
                    unit = not (first and u < 1)
                    if unit and not odd:
                        do.neg_max(n, r)
                    if not odd and u % 4 == 1:
                        b = (u - 9) // 4
                        if b >= 0:
                            do.normalise(i, b)
                        elif not first:
                            do.normalise(i - 1, SB + b)
                    if mixer:
                        mixer_at(i + 1, p)
                    if ffn:
                        ffn_at(i - 1, p)
                    if p == 16:
                        residual(i)
                    if unit and odd:
                        do.probs(n, r)
                st.restart()

            def mixer_at(k, p):
                if p == 0:
                    do.rms_factor(k)
                    do.rms_scale(k)
                if p == 3:
                    do.clip_xn(k)
                if p == 6:
                    do.cap(zm, ze, "ze_ready", "zm_ready", k)
                if p == 7:
                    do.silu(k)
                if p == 8:
                    do.cap(dtm, dte, "dte_ready", "dtm_ready", k)
                if p == 10:
                    do.clip_dt(k)
                if p == 10:
                    do.rope(k)
                if p == 11:
                    do.step_input(k)
                if p == 12:
                    do.cap(gm, ge, "ge_ready", "gm_ready", k)
                if p == 12:
                    do.decay(k)
                if p == 14:
                    do.chunk_decay(k)
                if p == 13:
                    do.grow(k)
                if p == 15:
                    do.chunk_out(k)
                if p == 16:
                    do.carry(k)
                if p == 19:
                    do.gated(k)
                if p == 21:
                    do.negative_mean(0, k)
                if p == 22:
                    do.layernorm(0, k)

            def ffn_at(k, p):
                if p == 13:
                    do.negative_mean(1, k)
                if p == 14:
                    do.layernorm(1, k)
                if p == 16:
                    clip_x2(k)
                if p in (20, 21, 22, 23):
                    clip_hidden(k, p - 20)
                if p == 28:
                    do.negative_mean(2, k)
                if p == 28:
                    do.layernorm(2, k)

            setup()
            st.restart()
            body(0, True, False)
            with g.Fori(1, NBLK - 1) as i:
                body(i, False, False)
            body(NBLK - 1, False, True)

        @block.vector
        def _(v):
            st = Steps(v, q["dve_steps"], q["dve_held"])
            do = Products(v, st)

            def top_rounds(n, r, rounds):
                if 0 in rounds:
                    st.hold(q["scores_copied"], n + 1)
                for rd in rounds:
                    base = st.n
                    for j in range(HG):
                        src = sc_sb[:, r, j, :] if rd == 0 else rest[:, r, j, :]
                        if rd > 0:
                            st.wait(mr[j])
                        mx8[j] = st.done(v.max(top[:, r, j, 8 * rd:8 * rd + 8], src))
                    for j in range(HG):
                        src = sc_sb[:, r, j, :] if rd == 0 else rest[:, r, j, :]
                        st.wait(mx8[j])
                        ins = v.match_replace(rest[:, r, j, :], top[:, r, j, 8 * rd:8 * rd + 8], src, TAKEN)
                        if rd == ROUNDS - 1 and j == HG - 1:
                            ins.then_inc(q["topk_done"], 1)
                        else:
                            mr[j] = st.done(ins)

            mr, mx8 = [0] * HG, [0] * HG

            def moments(n, source, src, k, which=ALL, first=""):
                v.wait_ge(q[first + source], made(k, first))
                done = [st.done(v.bn_stats(bst[n][:, b, :], src[:, S * b:S * (b + 1)])) for b in which]
                for b in which:
                    st.wait(done[b - which[0]])
                    ins = v.bn_aggr(mv[n][:, b, :], bst[n][:, b, :])
                    if b < which[-1]:
                        st.done(ins)
                ins.then_inc(q[first + f"stats{n}_ready"], 1)

            def norm_offset(n, k, count, which=ALL, first=""):
                if not first:
                    wait(v, q[f"ln{n}_ready"], k)
                v.wait_ge(q[first + "rstd_ready"], count)
                part = slice(which[0], which[-1] + 1)
                v.scalar_tensor_tensor(nb[n][:, part], mv[n][:, part, 0], -1.0, rs[n][:, part], ALU.mult, ALU.mult)\
                    .then_inc(q[first + f"ln{n}_ready"], 1)

            def convolve_first():
                v.wait_ge(q["xn_ready"], 1)
                steps = (zl, zs, zl, z)
                st.done(v.tensor_scalar(seqs(steps[0]), xnp[:, :, 0:S], convw[:, 0:1], convb, ALU.mult, ALU.add))
                for j in range(1, K):
                    st.wait()
                    ins = v.scalar_tensor_tensor(seqs(steps[j]), xnp[:, :, j:j + S], convw[:, j:j + 1],
                                                 seqs(steps[j - 1]), ALU.mult, ALU.add)
                    if j < K - 1:
                        st.done(ins)
                ins.then_inc(q["conv_ready"], 1)

            def scan(ready, out_, keep_, in_, sem_, k):
                v.wait_ge(q[ready], k + 1)
                v.tensor_tensor_scan(out_, keep_, in_, 0.0, ALU.mult, ALU.add).then_inc(q[sem_], 1)

            def running_dt(k):
                scan("dt_ready", cum[:, :], keep[:, :], dt_[:, :], "cum_ready", k)

            def running_chunk_dt(k):
                scan("cc_ready", cdr[:, :], keepc[:, :], chunks(cc)[:, :, CHUNK - 1], "cdr_ready", k)

            def running_state(k):
                scan("w_ready", cs[:, :], keep[:, :], w_[:, :], "cs_ready", k)

            def running_carry(k):
                scan("seeds_ready", cse[:, :], keepc[:, :], seeds[:, :], "cse_ready", k)

            def inverse(k, b):
                v.wait_ge(q["ctx_copied"], SB * k + b + 1)
                v.reciprocal(rden[:, b % 2, :], ctxo[:, b % 2, :, DH]).then_inc(q["rden_ready"], 1)

            def quantise_x2(k, which=ALL, early=""):
                part = slice(which[0], which[-1] + 1)
                v.wait_ge(q[early + "x2_ready"], made(k, early))
                if not early:
                    v.wait_ge(q["xq_ready"], k)
                st.done(v.tensor_scalar(q1[:, part, :], x2[:, part, :], 127.0 / 16, -8.0, ALU.min, ALU.max))
                st.wait()
                st.done(v.tensor_scalar(q2[:, part, :], q1[:, part, :], 16.0, MAGIC, ALU.mult, ALU.add))
                st.wait()
                v.tensor_scalar(xq[:, part, :], q2[:, part, :], -MAGIC, None, ALU.add)\
                    .then_inc(q[early + "xq_ready"], 1)

            def quantise_hidden(k, c, which=ALL, early=""):
                base = 0 if early else FC * k
                v.wait_ge(q[early + "relu_ready"], base + c + 1)
                if not early:
                    v.wait_ge(q["hq_ready"], base + c)
                st.done(v.tensor_scalar(hu[:, c, span(which)], hr[:, c, span(which)], 127.0, MAGIC,
                                        ALU.min, ALU.add))
                st.wait()
                v.tensor_scalar(hq[:, c, span(which)], hu[:, c, span(which)], -MAGIC, None, ALU.add)\
                    .then_inc(q[early + "hq_ready"], 1)

            def mixer_at(k, p):
                if p == 13:
                    running_dt(k)
                if p == 15:
                    running_chunk_dt(k)
                if p == 16:
                    running_state(k)
                if p == 18:
                    running_carry(k)

            def body(i, first, last):
                for p in range(2 * UNITS):
                    u, odd = divmod(p, 2)
                    if odd and u % 4 == 0:
                        b = (u - 8) // 4
                        if b >= 0:
                            inverse(i, b)
                        elif not first:
                            inverse(i - 1, SB + b)
                    if not last:
                        mixer_at(i + 1, p)
                    half = ROUNDS // 2
                    top_rounds(UNITS * i + u, u % 4, range(half, ROUNDS) if odd else range(half))
                st.restart()

            def quantise_weight(src, t, u, out_, factor=1.0):
                st.done(v.tensor_scalar(t, src, 64.0, 127.0, ALU.mult, ALU.min))
                st.wait()
                st.done(v.tensor_scalar(u, t, -128.0, MAGIC, ALU.max, ALU.add))
                st.wait()
                st.done(v.tensor_scalar(out_, u, -MAGIC, factor, ALU.add, ALU.mult))

            v.wait_ge(q["x_loaded"], 16)
            do.rms_scale(0)
            v.wait_ge(q["tables_loaded"], 32)
            for j in range(K):
                st.done(v.tensor_scalar(convdiag[:, j, :], ident, convw[:, j:j + 1], None, ALU.mult))
            st.done(v.tensor_scalar(ident2[:, :], ident, 2.0, None, ALU.mult))
            st.done(v.tensor_scalar(ident1024[:, :], ident, 1024.0, None, ALU.mult))
            st.done(v.tensor_copy(ident16[:, :], ident))
            st.done(v.tensor_tensor(mixkron[:, :, :], mixrep.unsqueeze(2).broadcast_to([P, H, DH]),
                                    cst[:, C_HD:C_HD + DH].unsqueeze(1).broadcast_to([P, H, DH]), ALU.mult))
            st.done(v.tensor_scalar(ncb[:, :], convb, -1.0, None, ALU.mult))
            st.done(v.tensor_scalar(bkmask[:, :], cst[:, C_KM:C_KM + HG], bk_sb, None, ALU.mult))
            v.wait_ge(q["in_w_loaded"], 16)
            wv = win_sb[:, D:2 * D].rearrange("p (h d) -> p h d", h=H)
            st.done(v.tensor_copy(wvswap[:, :, 0:DH // 2], wv[:, :, DH // 2:DH]))
            st.done(v.tensor_copy(wvswap[:, :, DH // 2:DH], wv[:, :, 0:DH // 2]))
            st.wait()
            v.nop().then_inc(q["setup_done"], 1)
            v.wait_ge(q["masks_set"], 1)
            do.clip_xn(0)
            convolve_first()
            do.cap(zm, ze, "ze_ready", "zm_ready", 0)
            do.silu(0)
            v.wait_ge(q["ffn_w_loaded"], 48)
            quantise_weight(w1_sb[:, :, :], w1_t[:, :, :], w1_u[:, :, :], w1q[:, :, :])
            quantise_weight(w2_sb[:, :], w2_t[:, :], w2_u[:, :], w2q[:, :])
            quantise_weight(vec[:, V_B1:V_B1 + FC], b1_t[:, :], b1_u[:, :], b1_s[:, :], 0.25)
            quantise_weight(b2_sb[:, :], b2_t[:, :], b2_u[:, :], b2q[:, :], 16.0)
            st.wait()
            v.nop().then_inc(q["ffn_quant"], 1)
            do.cap(dtm, dte, "dte_ready", "dtm_ready", 0)
            do.clip_dt(0)
            running_dt(0)
            do.decay(0)
            running_chunk_dt(0)
            do.chunk_decay(0)
            do.rope(0)
            do.step_input(0)
            do.cap(gm, ge, "ge_ready", "gm_ready", 0)
            do.grow(0)
            running_state(0)
            do.chunk_out(0)
            running_carry(0)
            do.carry(0)
            do.gated(0, FIRST, "first_")
            moments(0, "outp_ready", OUT_BANK["first_"], 0, FIRST, "first_")
            norm_offset(0, 0, 1, FIRST, "first_")
            do.gated(0, OTHERS)
            moments(0, "outp_ready", ps_mixC, 0, OTHERS)
            norm_offset(0, 0, 1, OTHERS)
            st.restart()
            body(0, True, False)
            with v.Fori(1, NBLK - 1) as i:
                body(i, False, False)
            body(NBLK - 1, False, True)
            n, k = UNITS * NBLK - 1, NBLK - 1
            v.wait_ge(q["negmax_ready"], n)
            do.neg_max(n, 3)
            v.wait_ge(q["on_ready"], SB * k + SB - 2)
            v.wait_ge(q["probs_ready"], n)
            inverse(k, SB - 2)
            do.normalise(k, SB - 2)
            do.probs(n, 3)
            inverse(k, SB - 1)
            do.normalise(k, SB - 1)
            E = (EARLY, "early_")
            moments(1, "attn_ready", ATTN_BANK["early_"], k, *E)
            norm_offset(1, k, 1, *E)
            moments(1, "attn_ready", ATTN_BANK[""], k, LATE)
            norm_offset(1, k, 2, LATE)
            quantise_x2(k, *E)
            quantise_x2(k, LATE)
            for c in range(FC):
                quantise_hidden(k, c, *E)
            for c in range(FC):
                quantise_hidden(k, c, LATE)
            moments(2, "out2_ready", EARLY_OUT, k, *E)
            moments(2, "out2_ready", LATE_OUT, k, LATE)
            norm_offset(2, k, 2, *E)
            norm_offset(2, k, 3, LATE)

        @block.scalar
        def _(a):
            st = Steps(a, q["act_steps"])

            def copy(out_, in_, bias=0.0, scale=1.0):
                return a.activation(out_, in_, ACT.Identity, bias=bias, scale=scale)

            def sigmoid(m, l, out_, ready):
                st.done(a.activation(l, m, ACT.Ln, bias=1.0))
                st.wait()
                a.activation(out_, l, ACT.Exp, scale=-1.0).then_inc(q[ready], 1)

            def apply_norm(n, src, out_, ready, which=ALL):
                for b in which:
                    ins = copy(out_[:, b, :], src[:, S * b:S * (b + 1)], bias=nb[n][:, b:b + 1],
                               scale=rs[n][:, b:b + 1])
                ins.then_inc(q[ready], 1)

            def sum_rows(n, made, src, k):
                a.wait_ge(q[made], k + 1)
                for b in range(SB):
                    ins = a.activation(junk[:, b, :], src[:, S * b:S * (b + 1)], ACT.Identity,
                                       accum_out=total[n][:, b:b + 1])
                ins.then_inc(q[f"sum{n}_ready"], 1)

            def sum_squares(n, src, k):
                a.wait_ge(q[f"nmean{n}_ready"], k + 1 - (n == 0))
                for b in range(SB):
                    ins = a.activation(junk[:, b, :], src[:, S * b:S * (b + 1)], ACT.Square,
                                       bias=nmean[n][:, b:b + 1], accum_out=spread[n][:, b:b + 1])
                ins.then_inc(q[f"stats{n}_ready"], 1)

            def inverse_root(out_, in_, eps, ready, scale=1.0, which=ALL):
                st.done(a.activation(ln_var[:, which[0]:which[-1] + 1], in_, ACT.Ln, bias=eps_sb[:, eps:eps + 1],
                                     scale=scale))
                st.wait()
                a.activation(out_[:, which[0]:which[-1] + 1], ln_var[:, which[0]:which[-1] + 1], ACT.Exp,
                             scale=-0.5).then_inc(q[ready], 1)

            def rstd(n, k, which=ALL, first=""):
                a.wait_ge(q[first + f"stats{n}_ready"], made(k, first))
                inverse_root(rs[n], mv[n][:, which[0]:which[-1] + 1, 1], n, first + "rstd_ready", which=which)

            def squares(k):
                a.wait_ge(q["x_loaded"], 16 * (k + 1))
                for b in range(SB):
                    ins = a.activation(junk[:, b, :], x_sb[:, b, :], ACT.Square, accum_out=ss[:, b:b + 1])
                ins.then_inc(q["ss_ready"], 1)

            def xn_copy(k):
                a.wait_ge(q["xsT_ready"], k + 1)
                copy(xnr[:, :], ps_mixA[:, :], scale=nscale).then_inc(q["xnr_ready"], 1)

            def conv_exp(k):
                a.wait_ge(q["conv_ready"], k + 1)
                a.activation(ze[:, :], ps_mixB[:, :], ACT.Exp, bias=ncb[:, :], scale=-1.0).then_inc(q["ze_ready"], 1)
                st.done(copy(z[:, :], ps_mixB[:, :], bias=convb))

            def conv_exp_first():
                a.wait_ge(q["conv_ready"], 1)
                a.activation(ze[:, :], z[:, :], ACT.Exp, scale=-1.0).then_inc(q["ze_ready"], 1)

            def conv_sigmoid(k):
                st.wait()
                a.wait_ge(q["zm_ready"], k + 1)
                sigmoid(zm[:, :], zl[:, :], zs[:, :], "sig_ready")

            def v_copy(k):
                a.wait_ge(q["vraw_ready"], k + 1)
                copy(v_sb[:, :], ps_mixB[:, :])
                copy(vw_sb[:, :], ps_mixC[:, :]).then_inc(q["v_copied"], 1)

            def dt_exp(k):
                a.wait_ge(q["dtraw_ready"], k + 1)
                a.activation(dte[:, :], ps_mixA[:, :], ACT.Exp, bias=dtb).then_inc(q["dte_ready"], 1)

            def softplus(k):
                a.wait_ge(q["dtm_ready"], k + 1)
                a.activation(dts[:, :], dtm[:, :], ACT.Ln, bias=1.0).then_inc(q["softplus_ready"], 1)

            def gate_exp(k):
                a.wait_ge(q["graw_ready"], k + 1)
                a.activation(ge[:, :], ps_mixB[:, :], ACT.Exp, scale=-1.0).then_inc(q["ge_ready"], 1)

            def gate_sigmoid(k):
                a.wait_ge(q["gm_ready"], k + 1)
                sigmoid(gm[:, :], gl[:, :], gate[:, :], "gate_ready")

            def decays(k):
                a.wait_ge(q["dst_ready"], k + 1)
                a.activation(egrow[:, :], dst[:, :], ACT.Exp).then_inc(q["egrow_ready"], 1)
                a.activation(edecay[:, :], dst[:, :], ACT.Exp, scale=-1.0).then_inc(q["edecay_ready"], 1)
                st.done(a.activation(ecar[:, :], cc[:, :], ACT.Exp, scale=-1.0))

            def chunk_exps(k):
                a.wait_ge(q["cn_ready"], k + 1)
                st.done(a.activation(eM[:, :], cn[:, :], ACT.Exp))
                st.done(a.activation(enM[:, :], cn[:, :], ACT.Exp, scale=-1.0))
                st.wait()
                a.nop().then_inc(q["em_ready"], 1)

            def mx_copy(k, which=ALL, first=""):
                a.wait_ge(q[first + "mix_ready"], k + 1)
                copy(mx[:, span(which)], MIX_BANK[first][:, span(which)]).then_inc(q[first + "mx_ready"], 1)

            def x1_apply(k, which=ALL, first=""):
                wait(a, q["x1h_ready"], k)
                a.wait_ge(q[first + "ln0_ready"], k + 1)
                apply_norm(0, OUT_BANK[first], x1, first + "x1_ready", which)

            def x1T_copy(k, which=ALL, first=""):
                a.wait_ge(q[first + "x1T_ready"], k + 1)
                copy(x1T[:, span(which)], TURN_BANK[first][:, span(which)]).then_inc(q[first + "x1T_copied"], 1)

            def ctxT_copy(k, src=ps_mixC):
                wait(a, q["vps_ready"], k)
                a.wait_ge(q["ctxT_ready"], k + 1)
                copy(ctxT[:, :], src[:, :]).then_inc(q["ctxT_copied"], 1)

            def q_copy(k, src=ps_mixA, which=ALL, first=""):
                wait(a, q["scores_ready"], UNITS * k)
                a.wait_ge(q[first + "qraw_ready"], k + 1)
                copy(qT[:, span(which)], src[:, span(which)], bias=bq_sb).then_inc(q[first + "q_ready"], 1)

            def k_copy(k, src=ps_mixB):
                a.wait_ge(q["kraw_ready"], k + 1)
                for j in range(HG):
                    ins = copy(kmaskT[:, :, j, :], seqs(src), bias=bkmask[:, j:j + 1],
                               scale=cst[:, C_KM + j:C_KM + j + 1])
                ins.then_inc(q["k_ready"], 1)

            def v_attn_copy(k):
                wait(a, q["pv_done"], UNITS * k)
                a.wait_ge(q["vps_ready"], k + 1)
                copy(vaug[:, :, :, 0:DH], ps_ffnA.rearrange("p (b h d) -> p b h d", b=SB, h=H))\
                    .then_inc(q["v_ready"], 1)

            def scores_copy(n, r):
                wait(a, q["exps_ready"], n - 3)
                a.wait_ge(q["scores_ready"], n + 1)
                copy(sc_sb[:, r, :, :], ps_scores.rearrange("p (j s) -> p j s", j=HG))\
                    .then_inc(q["scores_copied"], 1)

            def exps(n, r):
                wait(a, q["probs_ready"], n - 1)
                a.wait_ge(q["negmax_ready"], n + 1)
                for j in range(HG):
                    ins = a.activation(ex[:, r % 2, j, :], sc_sb[:, r, j, :], ACT.Exp,
                                       bias=negmax[:, r, j:j + 1], scale=SCALE)
                for j in range(HG):
                    ins = a.activation(exr[:, r % 2, j, :], rest[:, r, j, :], ACT.Exp,
                                       bias=negmax[:, r, j:j + 1], scale=SCALE)
                ins.then_inc(q["exps_ready"], 1)

            def probsT_copy(n, r):
                wait(a, q["pv_done"], n - 1)
                a.wait_ge(q["probsT_ready"], n + 1)
                copy(prT[:, r % 2, :, :], ps_probsT.rearrange("p (j s) -> p j s", j=HG))\
                    .then_inc(q["probsT_copied"], 1)

            def ctx_copy(k, b):
                wait(a, q["on_ready"], SB * k + b - 1)
                a.wait_ge(q["pv_done"], UNITS * k + NG * (b + 1))
                copy(ctxo[:, b % 2, :, :], ps_ctx[:, 0:H * (DH + 1)].rearrange("p (h d) -> p h d", h=H))\
                    .then_inc(q["ctx_copied"], 1)

            def oT_copy(k, which=ALL, early=""):
                a.wait_ge(q[early + "onT_ready"], made(k, early))
                copy(oT[:, span(which)], HEADS_BANK[early][:, span(which)], bias=bv_sb)\
                    .then_inc(q[early + "oT_copied"], 1)

            def x2_apply(k, which=ALL, early=""):
                a.wait_ge(q[early + "ln1_ready"], made(k, early))
                apply_norm(1, ATTN_BANK[early], x2, early + "x2_ready", which)

            def x2_round(k):
                a.wait_ge(q["q1_ready"], k + 1)
                st.done(copy(q2[:, :, :], q1[:, :, :], bias=magic[:, :], scale=16.0))
                st.wait()
                copy(xq[:, :, :], q2[:, :, :], bias=minus_magic[:, :]).then_inc(q["xq_ready"], 1)

            def xqT_copy(k, which=ALL, early=""):
                a.wait_ge(q[early + "xqT_ready"], made(k, early))
                copy(xqT[:, span(which)], XQ_BANK[early][:, span(which)]).then_inc(q[early + "xqT_copied"], 1)

            def relu(k, c, bank=None, which=ALL, early=""):
                a.wait_ge(q[early + "h_ready"], (0 if early else FC * k) + c + 1)
                a.activation(hr[:, c, span(which)], (bank or (ps_ffnB, ps_ffnA)[c % 2])[:, span(which)], ACT.Relu,
                             bias=b1_s[:, c:c + 1], scale=1.0 / 64).then_inc(q[early + "relu_ready"], 1)

            def h_round(k, c):
                a.wait_ge(q["hu_ready"], FC * k + c + 1)
                copy(hq[:, c, :], hu[:, c, :], bias=minus_magic[:, :]).then_inc(q["hq_ready"], 1)

            def out_apply(k, src=ps_ffnA, which=ALL, early=""):
                a.wait_ge(q["out_free"], 16 * (k + 1))
                a.wait_ge(q[early + "ln2_ready"], made(k, early))
                apply_norm(2, src, out_sb, early + "out_ready", which)

            def mixer_at(k, p):
                if p == 0:
                    squares(k)
                if p == 2:
                    xn_copy(k)
                if p == 5:
                    conv_exp(k)
                if p == 6:
                    conv_sigmoid(k)
                if p == 7:
                    dt_exp(k)
                if p == 9:
                    softplus(k)
                if p == 9:
                    v_copy(k)
                if p == 10:
                    gate_exp(k)
                if p == 13:
                    gate_sigmoid(k)
                if p == 13:
                    decays(k)
                if p == 15:
                    chunk_exps(k)
                if p == 13:
                    ctxT_copy(k)
                if p == 19:
                    mx_copy(k)
                if p == 21:
                    sum_rows(0, "outp_ready", ps_mixC, k)
                if p == 22:
                    sum_squares(0, ps_mixC, k)
                if p == 23:
                    x1_apply(k)
                if p == 24:
                    x1T_copy(k)
                if p == 28:
                    q_copy(k)
                if p == 26:
                    k_copy(k)

            def ffn_at(k, p):
                if p == 11:
                    oT_copy(k)
                if p == 13:
                    sum_rows(1, "attn_ready", ps_ffnB, k)
                if p == 14:
                    sum_squares(1, ps_ffnB, k)
                if p == 15:
                    x2_apply(k)
                if p == 17:
                    x2_round(k)
                if p == 18:
                    xqT_copy(k)
                if p in (19, 20, 21, 22):
                    relu(k, p - 19)
                if p in (21, 22, 23, 24):
                    h_round(k, p - 21)
                if p == 27:
                    sum_rows(2, "out2_ready", ps_ffnA, k)
                if p == 28:
                    sum_squares(2, ps_ffnA, k)
                if p == 29:
                    out_apply(k)

            def body(i, first, last):
                for p in range(2 * UNITS):
                    u, odd = divmod(p, 2)
                    n = UNITS * i + u
                    if not odd and u < UNITS - 2:
                        scores_copy(n + 2, (u + 2) % 4)
                    if p == 6:
                        v_attn_copy(i)
                    if not last:
                        mixer_at(i + 1, p)
                    if not first:
                        ffn_at(i - 1, p)
                    if not odd:
                        if not (first and u < 1):
                            exps(n - 1, (u - 1) % 4)
                    else:
                        if not (first and u < 2):
                            probsT_copy(n - 2, (u - 2) % 4)
                        if u % 4 == 2:
                            b = (u - 6) // 4
                            if b >= 0:
                                ctx_copy(i, b)
                            elif not first:
                                ctx_copy(i - 1, SB - 1)
                    if u >= UNITS - 2 and not odd and not last:
                        first_unit = u - (UNITS - 2)
                        scores_copy(UNITS * (i + 1) + first_unit, first_unit)
                st.restart()

            a.preload_act_table_set("natural_log_exp_and_others")
            a.dma_start(cst[:, :], const[:, :]).then_inc(q["tables_loaded"], 16)
            a.dma_start(vec[:, :], vectors[:, :]).then_inc(q["tables_loaded"], 16)
            squares(0)
            a.wait_ge(q["masks_set"], 1)
            a.wait_ge(q["ss_ready"], 1)
            inverse_root(rms, ss[:, :], 3, "rms_ready", 1.0 / D)
            a.dma_start(w1_sb[:, :, :], w1.rearrange("(c p) d -> p c d", c=FC)).then_inc(q["ffn_w_loaded"], 16)
            a.dma_start(w2_sb[:, :], w2[:, :]).then_inc(q["ffn_w_loaded"], 16)
            a.dma_start(b2_sb[:, :], b2.rearrange("(o d) -> o d", o=1)).then_inc(q["ffn_w_loaded"], 16)
            a.wait_ge(q["tables_loaded"], 32)
            xn_copy(0)
            conv_exp_first()
            conv_sigmoid(0)
            dt_exp(0)
            softplus(0)
            v_copy(0)
            decays(0)
            chunk_exps(0)
            gate_exp(0)
            ctxT_copy(0, ps_ffnA)
            gate_sigmoid(0)
            k_copy(0, ps_ffnB)
            mx_copy(0, FIRST, "first_")
            rstd(0, 0, FIRST, "first_")
            x1_apply(0, FIRST, "first_")
            mx_copy(0, OTHERS)
            x1T_copy(0, FIRST, "first_")
            q_copy(0, ps_mixB, FIRST, "first_")
            rstd(0, 0, OTHERS)
            scores_copy(0, 0)
            x1_apply(0, OTHERS)
            scores_copy(1, 1)
            x1T_copy(0, OTHERS)
            q_copy(0, ps_mixB, OTHERS)
            a.wait_ge(q["ffn_wT"], 1)
            copy(w1T[:, :, :], ps_ffnA16[:, 0:HID].rearrange("p (c d) -> p c d", c=FC))
            copy(w2T[:, :, :], ps_ffnB16[:, 0:HID].rearrange("p (c d) -> p c d", c=FC)).then_inc(q["ffn_w"], 1)
            st.restart()
            body(0, True, False)
            with a.Fori(1, NBLK - 1) as i:
                body(i, False, False)
            body(NBLK - 1, False, True)
            n, k = UNITS * NBLK, NBLK - 1
            E = (EARLY, "early_")
            probsT_copy(n - 2, 2)
            exps(n - 1, 3)
            oT_copy(k, *E)
            probsT_copy(n - 1, 3)
            ctx_copy(k, SB - 1)
            oT_copy(k, LATE)
            rstd(1, k, *E)
            x2_apply(k, *E)
            rstd(1, k, LATE)
            x2_apply(k, LATE)
            xqT_copy(k, *E)
            for c in range(FC):
                relu(k, c, EARLY_HIDDEN[c], *E)
                if c == 0:
                    xqT_copy(k, LATE)
            for c in range(FC):
                relu(k, c, LATE_HIDDEN[c], LATE)
            rstd(2, k, *E)
            rstd(2, k, LATE)
            out_apply(k, EARLY_OUT, *E)
            out_apply(k, LATE_OUT, LATE)

        @block.tensor
        def _(t):
            def tokens(b):
                return slice(S * b, S * (b + 1))

            def mm(out_, lhsT, rhs, start=True, stop=True):
                return t.matmul(out_, lhsT, rhs, start=start, stop=stop)

            def xs_turn(k):
                wait(t, q["q_ready"], k)
                t.wait_ge(q["xs_ready"], k + 1)
                for b in range(SB):
                    ins = t.transpose(ps_mixA[:, tokens(b)], xs[:, b, :], ident)
                ins.then_inc(q["xsT_ready"], 1)

            def conv(k):
                wait(t, q["k_ready"], k)
                t.wait_ge(q["xn_ready"], k + 1)
                for j in range(K):
                    ins = mm(seqs(ps_mixB), convdiag[:, j, :], xnp[:, :, j:j + S], start=(j == 0), stop=(j == K - 1))
                ins.then_inc(q["conv_ready"], 1)

            def project_dt(k):
                t.wait_ge(q["xc_ready"], k + 1)
                mm(ps_mixA[:, :], win_sb[:, 0:D], xc[:, :]).then_inc(q["dtraw_ready"], 1)

            def project_values(k):
                mm(ps_mixB[:, :], win_sb[:, D:2 * D], xc[:, :])
                mm(ps_mixC[:, :], wvswap.rearrange("p h d -> p (h d)"), xc[:, :]).then_inc(q["vraw_ready"], 1)

            def project_gate(k):
                t.wait_ge(q["v_copied"], k + 1)
                mm(ps_mixB[:, :], win_sb[:, 2 * D:3 * D], xc[:, :]).then_inc(q["graw_ready"], 1)

            def mix_heads(k, which=ALL, first=""):
                t.wait_ge(q["fin_ready"], k + 1)
                mm(MIX_BANK[first][:, span(which)], mixkron.rearrange("p h d -> p (h d)"), fin[:, span(which)])\
                    .then_inc(q[first + "mix_ready"], 1)

            def mixer_residual(k, which=ALL, first=""):
                t.wait_ge(q["ctxT_copied"], k + 1)
                mm(OUT_BANK[first][:, span(which)], ident2[:, :], x_sb.rearrange("p b d -> p (b d)")[:, span(which)],
                   stop=False)

            def project_out(k, which=ALL, first=""):
                t.wait_ge(q[first + "y_ready"], k + 1)
                for b in which:
                    ins = mm(OUT_BANK[first][:, tokens(b)], y[:, tokens(b)], wout_sb, start=False,
                             stop=(b == which[-1]))
                ins.then_inc(q[first + "outp_ready"], 1)

            def x1_turn(k, which=ALL, first=""):
                t.wait_ge(q[first + "x1_ready"], k + 1)
                for b in which:
                    ins = t.transpose(TURN_BANK[first][:, tokens(b)], x1[:, b, :], ident)
                ins.then_inc(q[first + "x1T_ready"], 1)

            def project_q(k, dst=ps_mixA, which=ALL, first=""):
                t.wait_ge(q[first + "x1T_copied"], k + 1)
                mm(dst[:, span(which)], wq_sb, x1T[:, span(which)]).then_inc(q[first + "qraw_ready"], 1)

            def ctx_turn(k, dst=ps_mixC):
                t.wait_ge(q["ctx_loaded"], 16 * (k + 1))
                if dst is ps_mixC:
                    t.wait_ge(q["v_copied"], k + 1)
                for b in range(SB):
                    ins = t.transpose(dst[:, tokens(b)], ctx_sb[:, b, :], ident)
                ins.then_inc(q["ctxT_ready"], 1)

            def project_k(k, dst=ps_mixB):
                t.wait_ge(q["ctxT_copied"], k + 1)
                if dst is ps_mixB:
                    t.wait_ge(q["ge_ready"], k + 1)
                mm(dst[:, :], wk_sb, ctxT[:, :]).then_inc(q["kraw_ready"], 1)

            def project_v(k):
                for b in range(SB):
                    ins = mm(ps_ffnA[:, tokens(b)], ctxT[:, tokens(b)], wv_sb)
                ins.then_inc(q["vps_ready"], 1)

            def scores(n, u):
                b, gr = divmod(u, NG)
                rows = slice(32 * gr, 32 * gr + 32)
                wait(t, q["scores_copied"], n)
                mm(ps_scores[:, :], qT[rows, tokens(b)], kmaskT[rows, b, :, :].rearrange("p j s -> p (j s)"))\
                    .then_inc(q["scores_ready"], 1)

            def probs_turn(n, r):
                wait(t, q["probsT_copied"], n)
                t.wait_ge(q["probs_ready"], n + 1)
                for j in range(HG):
                    ins = t.transpose(ps_probsT[:, tokens(j)], pr[:, r % 2, j, :], ident)
                ins.then_inc(q["probsT_ready"], 1)

            def times_v(n, u, k):
                b, gr = divmod(u, NG)
                if u == 0:
                    t.wait_ge(q["v_ready"], k + 1)
                if gr == 0:
                    wait(t, q["ctx_copied"], SB * k + b)
                t.wait_ge(q["probsT_copied"], n + 1)
                for j in range(HG):
                    h = HG * gr + j
                    ins = mm(ps_ctx[:, (DH + 1) * h:(DH + 1) * (h + 1)], prT[:, u % 2, j, :], vaug[:, b, h, :])
                ins.then_inc(q["pv_done"], 1)

            def on_turn(k, which=ALL, early=""):
                t.wait_ge(q["v_ready"], k + 2 if not isinstance(k, int) else min(k + 2, NBLK))
                t.wait_ge(q["on_ready"], SB * k + which[-1] + 1)
                for b in which:
                    ins = t.transpose(HEADS_BANK[early][:, tokens(b)], on[:, b, :, :].rearrange("p h d -> p (h d)"),
                                      ident)
                ins.then_inc(q[early + "onT_ready"], 1)

            def attn_residual(k, which=ALL, early=""):
                t.wait_ge(q["x1h_ready"], k + 1)
                mm(ATTN_BANK[early][:, span(which)], ident, x1h.rearrange("p b d -> p (b d)")[:, span(which)],
                   stop=False)

            def attn_out(k, which=ALL, early=""):
                t.wait_ge(q[early + "oT_copied"], made(k, early))
                for b in which:
                    ins = mm(ATTN_BANK[early][:, tokens(b)], oT[:, tokens(b)], wo_sb, start=False,
                             stop=(b == which[-1]))
                ins.then_inc(q[early + "attn_ready"], 1)

            def xq_turn(k, which=ALL, early=""):
                t.wait_ge(q[early + "xq_ready"], made(k, early))
                for b in which:
                    ins = t.transpose(XQ_BANK[early][:, tokens(b)], xq[:, b, :], ident16[:, :])
                ins.then_inc(q[early + "xqT_ready"], 1)

            def hidden(k, c, bank=None, which=ALL, early=""):
                if c == 0:
                    t.wait_ge(q[early + "xqT_copied"], made(k, early))
                if bank is None and c >= 2:
                    t.wait_ge(q["relu_ready"], FC * k + c - 1)
                if early and c == FC - 1:
                    t.wait_ge(q["early_relu_ready"], 1)
                mm((bank or (ps_ffnB, ps_ffnA)[c % 2])[:, span(which)], w1T[:, c, :], xqT[:, span(which)])\
                    .then_inc(q[early + "h_ready"], 1)

            def ffn_residual(k, bank, which=ALL, early=""):
                if bank is ps_ffnA:
                    t.wait_ge(q["relu_ready"], FC * (k + 1))
                if bank is LATE_OUT:
                    t.wait_ge(q["early_relu_ready"], FC)
                t.wait_ge(q[early + "x2_ready"], made(k, early))
                mm(bank[:, span(which)], ident1024[:, :], x2.rearrange("p b d -> p (b d)")[:, span(which)], stop=False)

            def ffn_out(k, bank, which=ALL, early=""):
                mm(seqs(bank)[:, which[0]:which[-1] + 1, :], ones_row[:, :],
                   b2q[:, :].unsqueeze(1).broadcast_to([1, len(which), D]), start=False, stop=False)
                for c in range(FC):
                    t.wait_ge(q[early + "hq_ready"], (0 if early else FC * k) + c + 1)
                    for b in which:
                        ins = mm(bank[:, tokens(b)], hq[:, c, tokens(b)], w2T[:, c, :],
                                 start=False, stop=(c == FC - 1 and b == which[-1]))
                ins.then_inc(q[early + "out2_ready"], 1)

            def mixer_at(k, p):
                if p == 2:
                    xs_turn(k)
                if p == 3:
                    conv(k)
                if p == 8:
                    project_dt(k)
                if p == 8:
                    project_values(k)
                if p == 10:
                    project_gate(k)
                if p == 12:
                    ctx_turn(k)
                if p == 16:
                    project_k(k)
                if p == 18:
                    mix_heads(k)
                if p == 20:
                    mixer_residual(k)
                    project_out(k)
                if p == 24:
                    x1_turn(k)
                if p == 26:
                    project_q(k)

            def ffn_at(k, p):
                if p == 11:
                    on_turn(k)
                if p == 11:
                    attn_residual(k)
                if p == 12:
                    attn_out(k)
                if p == 18:
                    xq_turn(k)
                if p in (18, 19, 20, 21):
                    hidden(k, p - 18)
                if p == 24:
                    ffn_residual(k, ps_ffnA)
                if p == 24:
                    ffn_out(k, ps_ffnA)

            def body(i, first, last):
                for p in range(2 * UNITS):
                    u, odd = divmod(p, 2)
                    n = UNITS * i + u
                    if not odd and u < UNITS - 2:
                        scores(n + 2, u + 2)
                    if odd:
                        if not (first and u < 2):
                            probs_turn(n - 2, (u - 2) % 4)
                        if u >= 3:
                            times_v(n - 3, u - 3, i)
                        elif not first:
                            times_v(n - 3, UNITS + u - 3, i - 1)
                    if p == 6:
                        project_v(i)
                    if not last:
                        mixer_at(i + 1, p)
                    if not first:
                        ffn_at(i - 1, p)
                    if u >= UNITS - 2 and not odd and not last:
                        first_unit = u - (UNITS - 2)
                        if first_unit == 0:
                            t.wait_ge(q["q_ready"], i + 2)
                            t.wait_ge(q["k_ready"], i + 2)
                        scores(UNITS * (i + 1) + first_unit, first_unit)

            t.wait_ge(q["tables_loaded"], 32)
            xs_turn(0)
            t.wait_ge(q["setup_done"], 1)
            t.wait_ge(q["w_loaded"], 16)
            ctx_turn(0, ps_ffnA)
            project_dt(0)
            project_values(0)
            project_gate(0)
            project_k(0, ps_ffnB)
            mix_heads(0, FIRST, "first_")
            mixer_residual(0, FIRST, "first_")
            project_out(0, FIRST, "first_")
            mix_heads(0, OTHERS)
            mixer_residual(0, OTHERS)
            x1_turn(0, FIRST, "first_")
            project_q(0, ps_mixB, FIRST, "first_")
            project_out(0, OTHERS)
            t.wait_ge(q["k_ready"], 1)
            t.wait_ge(q["first_q_ready"], 1)
            scores(0, 0)
            scores(1, 1)
            x1_turn(0, OTHERS)
            project_q(0, ps_mixB, OTHERS)
            t.wait_ge(q["ffn_quant"], 1)
            for c in range(FC):
                t.transpose(ps_ffnA16[:, tokens(c)], w1q[:, c, :], ident16[:, :])
            for c in range(FC):
                ins = t.transpose(ps_ffnB16[:, tokens(c)], w2q[:, tokens(c)], ident16[:, :])
            ins.then_inc(q["ffn_wT"], 1)
            t.wait_ge(q["ffn_w"], 1)
            body(0, True, False)
            with t.Fori(1, NBLK - 1) as i:
                body(i, False, False)
            body(NBLK - 1, False, True)
            n, k = UNITS * NBLK, NBLK - 1
            E = (EARLY, "early_")
            attn_residual(k, *E)
            probs_turn(n - 2, 2)
            times_v(n - 3, UNITS - 3, k)
            times_v(n - 2, UNITS - 2, k)
            on_turn(k, *E)
            probs_turn(n - 1, 3)
            times_v(n - 1, UNITS - 1, k)
            attn_out(k, *E)
            attn_residual(k, LATE)
            on_turn(k, LATE)
            attn_out(k, LATE)
            xq_turn(k, *E)
            xq_turn(k, LATE)
            for c in range(FC):
                hidden(k, c, EARLY_HIDDEN[c], *E)
            for c in range(FC):
                hidden(k, c, LATE_HIDDEN[c], LATE)
            ffn_residual(k, EARLY_OUT, *E)
            ffn_residual(k, LATE_OUT, LATE)
            ffn_out(k, EARLY_OUT, *E)
            ffn_out(k, LATE_OUT, LATE)


def kernel(**inputs):
    import numpy as _np
    import concourse.bacc as _bacc
    from concourse import mybir as _mybir
    from concourse.bass_utils import run_bass_kernel_spmd as _run

    def arr(name):
        return _np.asarray(inputs[name])

    vectors = _np.concatenate([
        arr('L0_attn_norm_scale')[:, None], arr('L0_attn_conv_w')[:, 0, :], arr('L0_attn_conv_b')[:, None],
        arr('L0_attn_dt_bias')[:, None], arr('L0_xattn_bq')[:, None], arr('L0_xattn_bk')[:, None],
        arr('L0_xattn_bv')[:, None], arr('L0_ffn_b1').reshape(FC, P).T,
        _np.repeat(arr('L0_attn_head_mix'), DH, axis=0),
        _np.broadcast_to(arr('L0_xattn_bo')[None, :], (P, D))], axis=1)
    weights = _np.concatenate([arr('L0_attn_out_proj_w'), arr('L0_xattn_Wq'), arr('L0_xattn_Wk'),
                               arr('L0_xattn_Wv'), arr('L0_xattn_Wo')], axis=1)
    laid_out = {'x': arr('x'), 'ctx': arr('ctx_1024'), 'const': constants(), 'vectors': vectors,
                'in_proj_w': arr('L0_attn_in_proj_w'), 'weights': weights, 'w1': arr('L0_ffn_w1'),
                'w2': arr('L0_ffn_w2'), 'b2': arr('L0_ffn_b2')}
    nc = _bacc.Bacc("TRN2", target_bir_lowering=False, num_devices=1)
    arrays, args = {}, []
    for name, a in laid_out.items():
        a = _np.ascontiguousarray(a)
        arrays[f"in_{name}"] = a
        args.append(nc.dram_tensor(f"in_{name}", a.shape, _mybir.dt.from_np(a.dtype), kind="ExternalInput").ap())
    args.append(nc.dram_tensor("out_0", (NSEQ, S, D), _mybir.dt.float32, kind="ExternalOutput").ap())
    decoder_kernel(nc, *args)
    r = _run(nc, [arrays], core_ids=[0])
    return r.results[0]["out_0"]
```
